# Optimizing a Trainium2 kernel written in Bass

```python
import numpy as np
import jax
import jax.numpy as jnp

def _softmax(x, axis=-1):
    return jax.nn.softmax(x, axis=axis)
def _gelu(x):
    return jax.nn.gelu(x, approximate=True)
def _silu(x):
    return jax.nn.silu(x)
def _sigmoid(x):
    return jax.nn.sigmoid(x)
def _layernorm(x, axis=-1, eps=1e-5):
    m = jnp.mean(x, axis=axis, keepdims=True)
    v = jnp.var(x, axis=axis, keepdims=True)
    return (x - m) / jnp.sqrt(v + eps)
def _scatter_add(tgt, idx, src, axis=0):
    return tgt.at[idx].add(src)
def _segment_sum(src, seg, n):
    return jax.ops.segment_sum(src, seg, n)

kernel_name = 'mk_conv_preact_d4_conv_nchw16_39d9e1'

def setup_inputs(seed: int = 0):
    np.random.seed(seed)
    _w = jnp.asarray
    def _rec_inputs():
        import jax
        import jax.numpy as jnp
        _gk = jax.random.key(seed)
        x = -7.109e-05 + 0.9999 * jax.random.normal(jax.random.fold_in(_gk, 1), (8, 16, 512, 512), jnp.float32)
        return x
    x = _rec_inputs()
    def _L0_conv_setup():
        import jax, jax.numpy as jnp
        import numpy as np
        B, C_IN, H, W = (16, 16, 512, 512)
        C_OUT, KH, KW = (16, 3, 3)
        N_EXPERTS = 3
        key = jax.random.key(seed)
        k1, k2, k3, k4 = jax.random.split(key, 4)
        x = jax.random.normal(k1, (B, C_IN, H, W), dtype=jnp.float32)
        fan_in = C_IN * KH * KW
        bound = np.sqrt(6.0 / fan_in)
        w_experts = jax.random.uniform(k2, (N_EXPERTS, C_OUT, C_IN, KH, KW), minval=-bound, maxval=bound, dtype=jnp.float32)
        bias = jnp.zeros((C_OUT,), dtype=jnp.float32)
        fc_bound = 1.0 / np.sqrt(C_IN)
        fc_w = jax.random.uniform(k3, (N_EXPERTS, C_IN), minval=-fc_bound, maxval=fc_bound, dtype=jnp.float32)
        fc_b = jnp.zeros((N_EXPERTS,), dtype=jnp.float32)
        return {'x': x, 'w_experts': w_experts, 'bias': bias, 'fc_w': fc_w, 'fc_b': fc_b}
    _L0_conv_all = _L0_conv_setup()
    _L0_conv_in = {k: v for k, v in _L0_conv_all.items() if k in ('w_experts', 'bias', 'fc_w', 'fc_b', )}
    del _L0_conv_all

    def _L1_conv_setup():
        import jax, jax.numpy as jnp
        import numpy as np
        K_SIZE = 3
        PAD = K_SIZE // 2

        def _diag_L(n, k):
            half = k // 2
            d = np.zeros(n, dtype=np.float32)
            d[:half] = 1.0
            d[n - half:] = 1.0
            if 2 * half < k:
                d[half] = 1.0
            return d

        def _circular_pad(w, H, W, k, p):
            w = jnp.roll(jnp.pad(jnp.flip(w, -1), ((0, 0), (0, 0), (0, 0), (0, W - k))), -p, axis=-1)
            w = jnp.roll(jnp.pad(jnp.flip(w, -2), ((0, 0), (0, 0), (0, H - k), (0, 0))), -p, axis=-2)
            return w
        key = jax.random.key(seed)
        kx, kw = jax.random.split(key)
        x = jax.random.normal(kx, (16, 16, 256, 256), dtype=jnp.float32)
        weight = jax.random.normal(kw, (16, 16, 3, 3), dtype=jnp.float32) * (2.0 / (16 * 9)) ** 0.5
        return {'x': x, 'weight': weight}
    _L1_conv_all = _L1_conv_setup()
    _L1_conv_in = {k: v for k, v in _L1_conv_all.items() if k in ('weight', )}
    del _L1_conv_all

    def _L2_conv_setup():
        import jax, jax.numpy as jnp
        import numpy as np
        K_SIZE = 3
        PAD = K_SIZE // 2

        def _diag_L(n, k):
            half = k // 2
            d = np.zeros(n, dtype=np.float32)
            d[:half] = 1.0
            d[n - half:] = 1.0
            if 2 * half < k:
                d[half] = 1.0
            return d

        def _circular_pad(w, H, W, k, p):
            w = jnp.roll(jnp.pad(jnp.flip(w, -1), ((0, 0), (0, 0), (0, 0), (0, W - k))), -p, axis=-1)
            w = jnp.roll(jnp.pad(jnp.flip(w, -2), ((0, 0), (0, 0), (0, H - k), (0, 0))), -p, axis=-2)
            return w
        key = jax.random.key(seed)
        kx, kw = jax.random.split(key)
        x = jax.random.normal(kx, (16, 16, 256, 256), dtype=jnp.float32)
        weight = jax.random.normal(kw, (16, 16, 3, 3), dtype=jnp.float32) * (2.0 / (16 * 9)) ** 0.5
        return {'x': x, 'weight': weight}
    _L2_conv_all = _L2_conv_setup()
    _L2_conv_in = {k: v for k, v in _L2_conv_all.items() if k in ('weight', )}
    del _L2_conv_all

    def _L3_conv_setup():
        import jax, jax.numpy as jnp
        import numpy as np
        KERNEL = 5
        PADDING = 2
        key = jax.random.key(seed)
        k1, k2 = jax.random.split(key)
        x = jax.random.normal(k1, (16, 16, 512, 512), dtype=jnp.float32)
        filter_w = jax.random.normal(k2, (16, 16, KERNEL), dtype=jnp.float32)
        return {'x': x, 'filter_w': filter_w}
    _L3_conv_all = _L3_conv_setup()
    _L3_conv_in = {k: v for k, v in _L3_conv_all.items() if k in ('filter_w', )}
    del _L3_conv_all

    return {
        "x": x,
        "L0_conv_w_experts": _L0_conv_in["w_experts"],
        "L0_conv_bias": _L0_conv_in["bias"],
        "L0_conv_fc_w": _L0_conv_in["fc_w"],
        "L0_conv_fc_b": _L0_conv_in["fc_b"],
        "L1_conv_weight": _L1_conv_in["weight"],
        "L2_conv_weight": _L2_conv_in["weight"],
        "L3_conv_filter_w": _L3_conv_in["filter_w"],
    }

def reference(x, L0_conv_w_experts, L0_conv_bias, L0_conv_fc_w, L0_conv_fc_b, L1_conv_weight, L2_conv_weight, L3_conv_filter_w):
    import jax
    import jax.numpy as jnp
    def _L0_conv_ref(x, w_experts, bias, fc_w, fc_b):
        import jax, jax.numpy as jnp
        import numpy as np
        B, C_IN, H, W = (16, 16, 512, 512)
        C_OUT, KH, KW = (16, 3, 3)
        N_EXPERTS = 3
        pooled = x.mean(axis=(2, 3))
        routing = jax.nn.softmax(pooled @ fc_w.T + fc_b, axis=1)
        kernels = jnp.einsum('bn,noihw->boihw', routing, w_experts)
        xp = jnp.pad(x, ((0, 0), (0, 0), (1, 1), (1, 1)), mode='reflect')

        def conv_one(xi, ki):
            return jax.lax.conv_general_dilated(xi[None], ki, window_strides=(1, 1), padding='VALID', dimension_numbers=('NCHW', 'OIHW', 'NCHW'))[0]
        out = jax.vmap(conv_one)(xp, kernels)
        return out + bias[None, :, None, None]

    def _L1_conv_ref(x, weight):
        import jax, jax.numpy as jnp
        import numpy as np
        K_SIZE = 3
        PAD = K_SIZE // 2

        def _diag_L(n, k):
            half = k // 2
            d = np.zeros(n, dtype=np.float32)
            d[:half] = 1.0
            d[n - half:] = 1.0
            if 2 * half < k:
                d[half] = 1.0
            return d

        def _circular_pad(w, H, W, k, p):
            w = jnp.roll(jnp.pad(jnp.flip(w, -1), ((0, 0), (0, 0), (0, 0), (0, W - k))), -p, axis=-1)
            w = jnp.roll(jnp.pad(jnp.flip(w, -2), ((0, 0), (0, 0), (0, H - k), (0, 0))), -p, axis=-2)
            return w
        B, Ci, H, W = x.shape
        k, p = (K_SIZE, PAD)
        w_pad = _circular_pad(weight, H, W, k, p)
        dL = jnp.asarray(np.outer(_diag_L(H, k), _diag_L(W, k)))
        Lw = jnp.fft.fft2(w_pad * dL)
        Kx = jnp.fft.ifft2(x, norm='ortho')
        z = jnp.einsum('oihw,bihw->bohw', Lw, Kx)
        y = jnp.fft.fft2(z, norm='ortho')
        return jnp.real(y).astype(x.dtype)

    def _L2_conv_ref(x, weight):
        import jax, jax.numpy as jnp
        import numpy as np
        K_SIZE = 3
        PAD = K_SIZE // 2

        def _diag_L(n, k):
            half = k // 2
            d = np.zeros(n, dtype=np.float32)
            d[:half] = 1.0
            d[n - half:] = 1.0
            if 2 * half < k:
                d[half] = 1.0
            return d

        def _circular_pad(w, H, W, k, p):
            w = jnp.roll(jnp.pad(jnp.flip(w, -1), ((0, 0), (0, 0), (0, 0), (0, W - k))), -p, axis=-1)
            w = jnp.roll(jnp.pad(jnp.flip(w, -2), ((0, 0), (0, 0), (0, H - k), (0, 0))), -p, axis=-2)
            return w
        B, Ci, H, W = x.shape
        k, p = (K_SIZE, PAD)
        w_pad = _circular_pad(weight, H, W, k, p)
        dL = jnp.asarray(np.outer(_diag_L(H, k), _diag_L(W, k)))
        Lw = jnp.fft.fft2(w_pad * dL)
        Kx = jnp.fft.ifft2(x, norm='ortho')
        z = jnp.einsum('oihw,bihw->bohw', Lw, Kx)
        y = jnp.fft.fft2(z, norm='ortho')
        return jnp.real(y).astype(x.dtype)

    def _L3_conv_ref(x, filter_w):
        import jax, jax.numpy as jnp
        import numpy as np
        KERNEL = 5
        PADDING = 2
        k = filter_w.shape[-1]
        kernel = filter_w[..., :, None] * jnp.eye(k, dtype=filter_w.dtype)
        out = jax.lax.conv_general_dilated(x, kernel, window_strides=(1, 1), padding=((PADDING, PADDING), (PADDING, PADDING)), dimension_numbers=('NCHW', 'OIHW', 'NCHW'))
        return out

    def _gn(v, G=8, eps=1e-5):
        B_, C_, H_, W_ = v.shape
        g = v.reshape(B_, G, C_ // G, H_, W_)
        m = jnp.mean(g, axis=(2, 3, 4), keepdims=True)
        s = jnp.var(g, axis=(2, 3, 4), keepdims=True)
        return ((g - m) / jnp.sqrt(s + eps)).reshape(v.shape)

    def _ln_c(v, eps=1e-6):
        m = jnp.mean(v, axis=1, keepdims=True)
        s = jnp.var(v, axis=1, keepdims=True)
        return (v - m) / jnp.sqrt(s + eps)

    def _ln_t(v, eps=1e-5):
        m = jnp.mean(v, axis=-1, keepdims=True)
        s = jnp.var(v, axis=-1, keepdims=True)
        return (v - m) / jnp.sqrt(s + eps)

    def _to_tokens(v):
        B_, C_, H_, W_ = v.shape
        return v.reshape(B_, C_, H_ * W_).transpose(0, 2, 1)
    def _from_tokens(t, like):
        B_, C_, H_, W_ = like.shape
        return t.transpose(0, 2, 1).reshape(B_, C_, H_, W_)

    x = x + _L0_conv_ref(_gn(x), L0_conv_w_experts, L0_conv_bias, L0_conv_fc_w, L0_conv_fc_b)
    x = x + _L1_conv_ref(_gn(x), L1_conv_weight)
    x = x + _L2_conv_ref(_gn(x), L2_conv_weight)
    x = x + _L3_conv_ref(_gn(x), L3_conv_filter_w)
    return x


_drawn_inputs = setup_inputs


def setup_inputs(seed=0):
    import zlib

    import numpy as np

    out = dict(_drawn_inputs(seed))
    spreads = {'L0_conv_bias': (0.0, 0.285), 'L0_conv_fc_b': (0.0, 0.307)}
    factors = {'L0_conv_fc_w': 198.039}
    for name, (base, spread) in spreads.items():
        noise = np.random.default_rng([zlib.crc32(name.encode()), seed]).standard_normal(out[name].shape)
        drawn = base * np.exp(spread * noise) if base else spread * noise
        out[name] = jnp.asarray(drawn.astype(out[name].dtype))
    for name, factor in factors.items():
        out[name] = (out[name] * factor).astype(out[name].dtype)
    return out
```

```python
import concourse.bass as bass
from concourse import mybir
from contextlib import ExitStack

N_IMG, C, H, W = 8, 16, 512, 512
P = 128
ROWS = P // C
BLOCKS = 4
UNITS = H // (ROWS * BLOCKS)
Q = 32
LAYERS = 4
PAD = 2
WP = W + 2 * PAD
SLOTS = 4
HALF = BLOCKS // 2
TAPS = [3, 3, 3, 5]
EXPERTS = 3
GROUP_EPS = 1e-5
SPLIT_SCALE = 64.0
ROW_ORDER = [0, 7, 1, 6, 2, 3, 4, 5]
SQUARE_PIECES = [(-1, -1), (8, -1), (-1, 0), (8, 0), (-1, 1), (8, 1)]
DIAGONAL_PIECES = [(-2, -2), (-1, -1), (8, 1), (9, 2), (-1, -2), (8, 2)]


def row_partition(row, rho):
    at = ROW_ORDER.index(row)
    return Q * ((at // 2 + rho) % 4) + C * (at % 2)


def build(nc, x, experts, bands, consts, small, out):
    fp32, fp16 = mybir.dt.float32, mybir.dt.float16
    ALU, ACT, AX = mybir.AluOpType, mybir.ActivationFunctionType, mybir.AxisListType
    NT = [t * P for t in TAPS]
    E_COLS = NT[0] + Q
    HALVES = [32, 33, 33, 32]
    HALVES_IMG = sum(HALVES)
    BAND_COLS = [BLOCKS * NT[1] + Q, BLOCKS * NT[2] + Q, BLOCKS * NT[3] + 2 * Q]
    DMA = 16

    ctx = ExitStack()
    with ctx:
        def sb(name, shape, dt):
            return ctx.enter_context(nc.sbuf_tensor(name, shape, dt))

        def sem(name):
            return ctx.enter_context(nc.semaphore(name))

        image = sb("image", [P, UNITS, BLOCKS, W], fp32)
        split = sb("split", [P, SLOTS, BLOCKS, 2, WP], fp16)
        halo = sb("halo", [P, 2, BLOCKS, 2, WP], fp16)
        normed = sb("normed", [P, 2, HALF, W], fp32)
        wrap = sb("wrap", [P, 2, WP], fp16)
        main_w = [sb(f"main_w{l}", [P, 2, BLOCKS, TAPS[l], P], fp16) for l in range(LAYERS)]
        halo_w = [sb(f"halo_w{l}", [P, 2, 1 + (l == 3), Q], fp16) for l in range(LAYERS)]
        stats = sb("stats", [P, UNITS, BLOCKS, 6], fp32)
        group_avg = sb("group_avg", [P, P], fp32)
        turns = sb("turns", [P, 3, P], fp32)
        ones = sb("ones", [P, P], fp32)
        tiny = sb("tiny", [P, 2 * EXPERTS + 1], fp32)
        agg = sb("agg", [P, 2], fp32)
        mean = sb("mean", [P, 1], fp32)
        dev = sb("dev", [P, 1], fp32)
        var_p = sb("var_p", [P, 1], fp32)
        var_eps = sb("var_eps", [P, 1], fp32)
        minus_half = sb("minus_half", [P, 1], fp32)
        root = sb("root", [P, 1], fp32)
        newton = sb("newton", [P, 2], fp32)
        scale = sb("scale", [P, 1], fp32)
        shift = sb("shift", [P, 1], fp32)
        zed = sb("zed", [P, EXPERTS], fp32)
        logits = sb("logits", [P, EXPERTS], fp32)
        top = sb("top", [P, 2], fp32)
        expd = sb("expd", [P, EXPERTS], fp32)
        total = sb("total", [P, 2], fp32)
        routing = sb("routing", [P, EXPERTS], fp32)
        psum = ctx.enter_context(nc.psum_tensor("psum", [P, 2, BLOCKS, W], fp32))

        fc_w, fc_b, bias = tiny[:, 0:EXPERTS], tiny[:, EXPERTS:2 * EXPERTS], tiny[:, 2 * EXPERTS:2 * EXPERTS + 1]
        last_slot = split[:, SLOTS - 1, :, :, :].rearrange("p b s w -> p (b s w)").bitcast(fp32)
        expert_w = last_slot[:, 0:EXPERTS * E_COLS].rearrange("p (e c) -> p e c", e=EXPERTS)
        mixed_w = last_slot[:, EXPERTS * E_COLS:(EXPERTS + 1) * E_COLS]
        mean_ps, var_ps, logit_ps = psum[:, 0, 0, 0:1], psum[:, 0, 1, 0:1], psum[:, 0, 2, 0:EXPERTS]
        stage = image[:, 12:15, :, :].rearrange("p u b w -> p (u b w)")

        x_in = [sem(f"x_in{k}") for k in range(4)]
        x_out = [sem(f"x_out{k}") for k in range(4)]
        halo_in = [sem(f"halo_in{k}") for k in range(4)]
        row0_in = sem("row0_in")
        consts_in = sem("consts_in")
        bands_in = sem("bands_in")
        experts_in = sem("experts_in")
        fixed_high = sem("fixed_high")
        fixed_low = sem("fixed_low")
        filled = sem("filled")
        high_done = sem("high_done")
        low_done = sem("low_done")
        split_done = sem("split_done")
        bias_done = sem("bias_done")
        conv_done = sem("conv_done")
        y_done = sem("y_done")
        stats_done = sem("stats_done")
        agg_done = sem("agg_done")
        mean_done = sem("mean_done")
        var_p_done = sem("var_p_done")
        var_done = sem("var_done")
        var_eps_done = sem("var_eps_done")
        root_done = sem("root_done")
        scalars_done = sem("scalars_done")
        zed_done = sem("zed_done")
        logit_done = sem("logit_done")
        top_done = sem("top_done")
        exp_done = sem("exp_done")
        mixed_done = sem("mixed_done")
        turned_done = sem("turned_done")
        mix_high = sem("mix_high")
        mix_low = sem("mix_low")
        dve_step = sem("dve_step")

        block = ctx.enter_context(nc.Block())

        def unit_no(img, layer, u):
            return img * (LAYERS * UNITS) + (layer * UNITS) + u

        def half_no(img, layer, u, h):
            return img * HALVES_IMG + u * 2 + (sum(HALVES[:layer]) + (HALVES[layer] - 32) + h)

        PIECES = 3 * [SQUARE_PIECES] + [DIAGONAL_PIECES]
        HALO_DMAS = [BLOCKS * len(pieces) for pieces in PIECES]

        def halo_level(img, layer, k, i):
            return img * (DMA * 4 * sum(HALO_DMAS)) + i * (DMA * HALO_DMAS[layer]) + \
                DMA * (4 * sum(HALO_DMAS[:layer]) + HALO_DMAS[layer])

        UNIT_DMAS = BLOCKS * 4

        def rows_of(t, img, i, k, rho, pair):
            first, second = ROW_ORDER[2 * pair], ROW_ORDER[2 * pair + 1]
            v = t[bass.ds(img, 1)].rearrange("o c (i k f r) w -> (o r) c i k f w", k=4, f=BLOCKS, r=ROWS)
            return v[first:second + 1:second - first, :, bass.ds(i, 1), k, rho, :]

        def image_rows(i, k, rho, pair):
            q = Q * ((pair + rho) % 4)
            v = image[:, :, :, :].rearrange("p (i k) b w -> p i k b w", k=4)
            return v[q:q + Q, bass.ds(i, 1), k, rho, :]

        @block.sync
        def _(sp):
            def load_unit(img, i, k):
                for rho in range(BLOCKS):
                    for pair in range(4):
                        sp.dma_start(image_rows(i, k, rho, pair), rows_of(x, img, i, k, rho, pair)).then_inc(x_in[k], DMA)

            def store_unit(img, i, k):
                for rho in range(BLOCKS):
                    for pair in range(4):
                        sp.dma_start(rows_of(out, img, i, k, rho, pair), image_rows(i, k, rho, pair)).then_inc(x_out[k], DMA)

            def row_pair(t, first, col):
                a = t[first:first + C, 0, col:col + W]
                return bass.AP(a.tensor, a.offset, [list(a.ap[0]), [1, WP + W]])

            def neighbour(layer, u, rho, row):
                k, side = u % 4, rho + row // ROWS
                if side < 0 and u == 0:
                    if layer == 0:
                        return split[:, k, 0, :, :], row_partition(-row, 0)
                    return wrap[:, :, :], (row_partition(7, 3) if layer < 3 else Q)
                if side >= BLOCKS and u == UNITS - 1:
                    if layer == 0:
                        return split[:, k, 3, :, :], row_partition(6, 3)
                    return wrap[:, :, :], (row_partition(0, 0) if layer < 3 else Q)
                return split[:, (k + side // BLOCKS) % SLOTS, side % BLOCKS, :, :], row_partition(row % ROWS, side % BLOCKS)

            def fetch_halo(layer, u, k):
                for rho in range(BLOCKS):
                    for n, (row, col) in enumerate(PIECES[layer]):
                        source, first = neighbour(layer, u, rho, row)
                        sp.dma_start(row_pair(halo[:, k % 2, rho, :, :], C * n, 0),
                                     row_pair(source, first, PAD + col)).then_inc(halo_in[k], DMA)

            def halo_step(img, layer, i, k, u):
                if u >= 2:
                    level = sp.to_reg(unit_no(img, layer, i * 4 + k - 1))
                    sp.wait_ge(bands_in, DMA)
                    sp.wait_ge(conv_done, level)
                ahead = half_no(img, layer, i * 4 + k + 1, 1) if u < UNITS - 1 else half_no(img, layer, UNITS, 0)
                level = sp.to_reg(ahead)
                sp.wait_ge(bands_in, DMA)
                sp.wait_ge(split_done, level)
                fetch_halo(layer, u, k)

            def store_step(img, i, k):
                level = sp.to_reg(unit_no(img, 3, i * 4 + k + 1))
                sp.wait_ge(bands_in, DMA)
                sp.wait_ge(y_done, level)
                store_unit(img, i, k)

            def reload_step(img, i, k):
                with sp.If(img < N_IMG - 1):
                    level = sp.to_reg(img * (4 * UNIT_DMAS * DMA) + (i * (UNIT_DMAS * DMA) + UNIT_DMAS * DMA))
                    sp.wait_ge(bands_in, DMA)
                    sp.wait_ge(x_out[k], level)
                    level = sp.to_reg(img * (4 * UNIT_DMAS * DMA) + (i * (UNIT_DMAS * DMA) + 4 * UNIT_DMAS * DMA))
                    sp.wait_ge(bands_in, DMA)
                    sp.wait_ge(x_in[k], level)
                    load_unit(nc.s_assert_within(img + 1, 1, N_IMG - 1, skip_runtime_bounds_check_because="only images before the last come here"), i, k)

            sp.dma_start(stage[:, 0:sum(BAND_COLS)], bands).then_inc(bands_in, DMA)
            sp.dma_start(group_avg[:, :], consts[:, 0:P]).then_inc(consts_in, DMA)
            sp.dma_start(turns[:, :, :].rearrange("p t m -> p (t m)"), consts[:, P:4 * P]).then_inc(consts_in, DMA)
            sp.dma_start(tiny[:, :], small).then_inc(consts_in, DMA)
            for u in range(UNITS):
                i, k = divmod(u, 4)
                if u >= 4:
                    sp.wait_ge(x_in[k], UNIT_DMAS * DMA * i)
                if u == 12:
                    sp.wait_ge(fixed_low, 6)
                load_unit(0, i, k)

            sp.wait_ge(filled, 2)
            with sp.Fori(0, N_IMG) as img:
                sp.wait_ge(agg_done, img * LAYERS + 1)
                sp.dma_start(expert_w, experts).then_inc(experts_in, DMA)
                for layer in range(3):
                    halo_step(img, layer, 0, 0, 0)
                    if layer > 0:
                        sp.dma_start(wrap[0:C, :, :], split[0:C, 0, 0, :, :]).then_inc(row0_in, DMA)
                        level = sp.to_reg(img * (2 * DMA) + layer * DMA)
                        sp.wait_ge(bands_in, DMA)
                        sp.wait_ge(row0_in, level)
                    for u in range(1, 4):
                        halo_step(img, layer, 0, u, u)
                    with sp.Fori(1, 3) as i:
                        for k in range(4):
                            halo_step(img, layer, i, k, 4 + k)
                    for u in range(12, UNITS):
                        halo_step(img, layer, 3, u % 4, u)
                halo_step(img, 3, 0, 0, 0)
                halo_step(img, 3, 0, 1, 1)
                for u in range(2, 4):
                    halo_step(img, 3, 0, u, u)
                    store_step(img, 0, u - 2)
                    if u == 3:
                        reload_step(img, 0, 0)
                with sp.Fori(1, 3) as i:
                    for k in range(4):
                        halo_step(img, 3, i, k, 4 + k)
                        store_step(img, *((i, k - 2) if k >= 2 else (i - 1, k + 2)))
                        reload_step(img, *((i, k - 3) if k >= 3 else (i - 1, k + 1)))
                for u in range(12, UNITS):
                    halo_step(img, 3, 3, u % 4, u)
                    store_step(img, *divmod(u - 2, 4))
                    reload_step(img, *divmod(u - 3, 4))
                for u in range(UNITS, UNITS + 2):
                    store_step(img, *divmod(u - 2, 4))
                    reload_step(img, *divmod(u - 3, 4))
                reload_step(img, *divmod(UNITS - 1, 4))
            for k in range(4):
                sp.wait_ge(x_out[k], N_IMG * 4 * UNIT_DMAS * DMA)

        @block.gpsimd
        def _(pool):
            def pad_columns(layer, t):
                def col(w, n=1):
                    return t[..., PAD + w:PAD + w + n] if len(t.shape) == 3 else t[:, :, :, PAD + w:PAD + w + n]
                if layer == 3:
                    nc.gpsimd.memset(col(-2, 2), 0.0)
                    return nc.gpsimd.memset(col(W, 2), 0.0)
                left, right = (1, W - 2) if layer == 0 else (W - 1, 0)
                nc.gpsimd.tensor_copy(col(-1), col(left))
                return nc.gpsimd.tensor_copy(col(W), col(right))

            def pad_half(img, layer, i, k, h):
                level = pool.to_reg(half_no(img, layer, i * 4 + k, h + 1))
                pool.wait_ge(filled, 2)
                pool.wait_ge(low_done, level)
                if layer == 0 and k == 3 and isinstance(i, int):
                    for col in (0, WP - 1):
                        nc.gpsimd.memset(split[:, k, HALF * h:HALF * h + HALF, :, col:col + 1], 0.0)
                pad_columns(layer, split[:, k, HALF * h:HALF * h + HALF, :, :]).then_inc(split_done, 1)

            nc.gpsimd.memset(wrap[:, :, :], 0.0)
            for col in (0, WP - PAD):
                nc.gpsimd.memset(split[:, :, :, :, col:col + PAD], 0.0)
            nc.gpsimd.memset(ones[:, :], 1.0)
            nc.gpsimd.memset(minus_half[:, :], -0.5).then_inc(filled, 1)
            pool.wait_ge(filled, 1)
            nc.gpsimd.memset(halo[3 * Q:4 * Q, :, :, :, :], 0.0).then_inc(filled, 1)
            pool.wait_ge(filled, 2)

            with pool.Fori(0, N_IMG) as img:
                for layer in range(LAYERS):
                    pool.wait_ge(var_eps_done, img * LAYERS + layer + 1)
                    nc.gpsimd.tensor_tensor(root[:, :], var_eps[:, :], minus_half[:, :], ALU.pow).then_inc(root_done, 1)
                    if layer in (1, 2):
                        level = pool.to_reg(half_no(img, layer, 0, 0))
                        pool.wait_ge(filled, 2)
                        pool.wait_ge(low_done, level)
                        pad_columns(layer, wrap[:, :, :]).then_inc(split_done, 1)
                    pad_half(img, layer, 0, 0, 0)
                    pad_half(img, layer, 0, 0, 1)
                    for k in range(1, 4):
                        for h in range(2):
                            pad_half(img, layer, 0, k, h)
                    with pool.Fori(1, 4) as i:
                        for k in range(4):
                            for h in range(2):
                                pad_half(img, layer, i, k, h)

        @block.scalar
        def _(act):
            def image_part(i, k, first, n):
                v = image[:, :, :, :].rearrange("p (i k) b w -> p (i k b) w", k=4)
                return v[:, bass.ds(i * (4 * BLOCKS) + (k * BLOCKS + first), n), :]

            def high_half(img, layer, i, k, h):
                n = (HALVES[layer] - 32 + 2 * k + h) % 2
                first_two = isinstance(i, int) and i == 0 and 2 * k + h + HALVES[layer] - 32 < 2
                if not first_two:
                    act.wait_ge(low_done, half_no(img, layer, i * 4 + k, h - 1))
                source = image_part(i, k, HALF * h, HALF)
                nc.scalar.activation(normed[:, n, :, :], source, ACT.Identity, bias=shift[:, :], scale=scale[:, :])
                nc.scalar.activation(split[:, k, HALF * h:HALF * h + HALF, 0, PAD:PAD + W], source, ACT.Identity,
                                     bias=shift[:, :], scale=scale[:, :]).then_inc(high_done, 1)

            def high_unit(img, layer, i, k, wait_slot):
                if wait_slot:
                    act.wait_ge(conv_done, unit_no(img, layer, i * 4 + k - 3))
                    back = (i - 1, k + 1) if k < 3 else (i, 0)
                    act.wait_ge(halo_in[(k + 1) % 4], halo_level(img, layer, (k + 1) % 4, back[0]))
                for h in range(2):
                    high_half(img, layer, i, k, h)
                if layer == 0:
                    level = act.to_reg(half_no(img, layer, i * 4 + k, 2))
                    act.wait_ge(bands_in, DMA)
                    act.wait_ge(high_done, level)
                    whole = image_part(i, k, 0, BLOCKS)
                    nc.scalar.activation(whole, whole, ACT.Identity, bias=bias, scale=1.0).then_inc(bias_done, 1)

            act.wait_ge(bands_in, DMA)
            at = 0
            for layer in (1, 2, 3):
                for t in (main_w[layer], halo_w[layer]):
                    v = t[:, 0].rearrange("p a t m -> p (a t m)") if t is main_w[layer] else t[:, 0].rearrange("p a m -> p (a m)")
                    n = v.shape[1]
                    nc.scalar.activation(v, stage[:, at:at + n], ACT.Copy, scale=SPLIT_SCALE).then_inc(fixed_high, 1)
                    at += n

            with act.Fori(0, N_IMG) as img:
                for layer in range(LAYERS):
                    act.wait_ge(scalars_done, img * LAYERS + layer + 1)
                    if layer in (1, 2):
                        source = image[3 * Q:4 * Q, UNITS - 1, BLOCKS - 1, :]
                        nc.scalar.activation(normed[3 * Q:4 * Q, 0, 0, :], source, ACT.Identity,
                                             bias=shift[3 * Q:4 * Q, :], scale=scale[3 * Q:4 * Q, :])
                        nc.scalar.activation(wrap[3 * Q:4 * Q, 0, PAD:PAD + W], source, ACT.Identity,
                                             bias=shift[3 * Q:4 * Q, :], scale=scale[3 * Q:4 * Q, :]).then_inc(high_done, 1)
                    for k in range(3):
                        high_unit(img, layer, 0, k, False)
                        if layer == 0 and k == 0:
                            act.wait_ge(top_done, img + 1)
                            nc.scalar.activation(expd[:, :], logits[:, :], ACT.Exp, bias=top[:, 1:2], scale=1.0,
                                                 accum_out=total[:, 0:1]).then_inc(exp_done, 1)
                    if layer == 0:
                        act.wait_ge(mixed_done, img + 1)
                        nc.scalar.copy(main_w[0][:, 0, 0].rearrange("p t m -> p (t m)"), mixed_w[:, 0:NT[0]]).then_inc(mix_high, 1)
                        nc.scalar.copy(halo_w[0][:, 0, 0], mixed_w[:, NT[0]:E_COLS]).then_inc(mix_high, 1)
                        for rho in range(1, BLOCKS):
                            act.wait_ge(turned_done, img * 3 + rho)
                            nc.scalar.copy(main_w[0][:, 0, rho].rearrange("p t m -> p (t m)"),
                                           psum[:, 1, rho - 1, 0:NT[0]]).then_inc(mix_high, 1)
                        act.wait_ge(mix_low, img * 5 + 5)
                    high_unit(img, layer, 0, 3, False)
                    with act.Fori(1, 4) as i:
                        for k in range(4):
                            high_unit(img, layer, i, k, True)

        @block.vector
        def _(dve):
            done = [0]

            def image_blocks(i, k, first, n):
                v = image[:, :, :, :].rearrange("p u b w -> p (u b) w")
                return v[:, bass.ds(i * (4 * BLOCKS) + (k * BLOCKS + first), n), :]

            def low_half(img, layer, i, k, h):
                n = (HALVES[layer] - 32 + 2 * k + h) % 2
                dve.wait_ge(high_done, half_no(img, layer, i * 4 + k, h + 1))
                nc.vector.tensor_tensor(split[:, k, HALF * h:HALF * h + HALF, 1, PAD:PAD + W], normed[:, n, :, :],
                                        split[:, k, HALF * h:HALF * h + HALF, 0, PAD:PAD + W],
                                        ALU.subtract).then_inc(low_done, 1)

            def low_unit(img, layer, i, k):
                low_half(img, layer, i, k, 0)
                low_half(img, layer, i, k, 1)

            def statistics(i, k):
                v = stats[:, :, :, :].rearrange("p u b s -> p (u b) s")
                for b in range(BLOCKS):
                    last = nc.vector.bn_stats(v[:, bass.ds(i * (4 * BLOCKS) + (k * BLOCKS + b), 1), :].rearrange("p o s -> p (o s)"),
                                              image_blocks(i, k, b, 1).rearrange("p o w -> p (o w)"))
                last.then_inc(stats_done, 1)

            def output_unit(img, layer, i, k):
                dve.wait_ge(conv_done, unit_no(img, layer, i * 4 + k + 1))
                if layer == 0:
                    dve.wait_ge(bias_done, img * UNITS + i * 4 + k + 1)
                x_unit = image_blocks(i, k, 0, BLOCKS)
                nc.vector.scalar_tensor_tensor(x_unit, psum[:, k % 2, :, :], 1.0 / SPLIT_SCALE ** 2, x_unit,
                                               ALU.mult, ALU.add).then_inc(y_done, 1)
                if layer < 3:
                    dve.wait_ge(y_done, unit_no(img, layer, i * 4 + k + 1))
                    statistics(i, k)

            def next_statistics(img, i, k):
                with dve.If(img < N_IMG - 1):
                    dve.wait_ge(x_in[k], img * (4 * UNIT_DMAS * DMA) + (i * (UNIT_DMAS * DMA) + 5 * UNIT_DMAS * DMA))
                    statistics(i, k)

            at, n_done = 0, 0
            for layer in (1, 2, 3):
                for t in (main_w[layer], halo_w[layer]):
                    names = "p a t m -> p (a t m)" if t is main_w[layer] else "p a m -> p (a m)"
                    high, low = t[:, 0].rearrange(names), t[:, 1].rearrange(names)
                    n, n_done = high.shape[1], n_done + 1
                    dve.wait_ge(fixed_high, n_done)
                    nc.vector.scalar_tensor_tensor(low, stage[:, at:at + n], SPLIT_SCALE, high,
                                                   ALU.mult, ALU.subtract).then_inc(fixed_low, 1)
                    at += n
            for u in range(UNITS):
                dve.wait_ge(x_in[u % 4], UNIT_DMAS * DMA * (u // 4 + 1))
                statistics(*divmod(u, 4))
            dve.wait_ge(consts_in, 3 * DMA)

            with dve.Fori(0, N_IMG) as img:
                done[0] = 0

                def step(instruction):
                    done[0] += 1
                    instruction.then_inc(dve_step, 1)
                    dve.wait_ge(dve_step, img * STEPS_ALL + done[0])

                STEPS_ALL = 4 * 4 + 6

                for layer in range(LAYERS):
                    level = dve.to_reg(img * (LAYERS * UNITS) + (layer + 1) * UNITS)
                    dve.wait_ge(consts_in, 3 * DMA)
                    dve.wait_ge(stats_done, level)
                    nc.vector.bn_aggr(agg[:, :], stats[:, :, :, :].rearrange("p u b s -> p (u b s)")).then_inc(agg_done, 1)
                    dve.wait_ge(mean_done, img * LAYERS + layer + 1)
                    nc.vector.tensor_copy(mean[:, :], mean_ps)
                    step(nc.vector.tensor_tensor(dev[:, :], agg[:, 0:1], mean_ps, ALU.subtract))
                    nc.vector.scalar_tensor_tensor(var_p[:, :], dev[:, :], dev[:, :], agg[:, 1:2],
                                                   ALU.mult, ALU.add).then_inc(var_p_done, 1)
                    dve.wait_ge(var_done, img * LAYERS + layer + 1)
                    nc.vector.tensor_scalar(var_eps[:, :], var_ps, GROUP_EPS, None, ALU.add).then_inc(var_eps_done, 1)
                    dve.wait_ge(root_done, img * LAYERS + layer + 1)
                    step(nc.vector.scalar_tensor_tensor(newton[:, 0:1], root[:, :], var_eps[:, :], root[:, :],
                                                        ALU.mult, ALU.mult))
                    step(nc.vector.tensor_scalar(newton[:, 1:2], newton[:, 0:1], -0.5, 1.5, ALU.mult, ALU.add))
                    step(nc.vector.scalar_tensor_tensor(scale[:, :], root[:, :], SPLIT_SCALE, newton[:, 1:2],
                                                        ALU.mult, ALU.mult))
                    nc.vector.scalar_tensor_tensor(shift[:, :], mean[:, :], -1.0, scale[:, :],
                                                   ALU.mult, ALU.mult).then_inc(scalars_done, 1)
                    if layer == 0:
                        nc.vector.tensor_scalar(zed[:, :], fc_w, dev[:, :], scale[:, :], ALU.mult, ALU.mult).then_inc(zed_done, 1)
                        low_unit(img, layer, 0, 0)
                        dve.wait_ge(logit_done, img + 1)
                        step(nc.vector.scalar_tensor_tensor(logits[:, :], logit_ps, 1.0 / (SPLIT_SCALE * ROWS), fc_b,
                                                            ALU.mult, ALU.add))
                        step(nc.vector.reduce_max(top[:, 0:1], logits[:, :], AX.X))
                        nc.vector.tensor_scalar(top[:, 1:2], top[:, 0:1], -1.0, None, ALU.mult).then_inc(top_done, 1)
                        dve.wait_ge(exp_done, img + 1)
                        step(nc.vector.reciprocal(total[:, 1:2], total[:, 0:1]))
                        step(nc.vector.tensor_scalar(routing[:, :], expd[:, :], total[:, 1:2], SPLIT_SCALE, ALU.mult, ALU.mult))
                        dve.wait_ge(experts_in, img * DMA + DMA)
                        step(nc.vector.tensor_scalar(mixed_w, expert_w[:, 0, :], routing[:, 0:1], None, ALU.mult))
                        step(nc.vector.scalar_tensor_tensor(mixed_w, expert_w[:, 1, :], routing[:, 1:2], mixed_w,
                                                            ALU.mult, ALU.add))
                        nc.vector.scalar_tensor_tensor(mixed_w, expert_w[:, 2, :], routing[:, 2:3], mixed_w,
                                                       ALU.mult, ALU.add).then_inc(mixed_done, 1)
                        low_unit(img, layer, 0, 1)
                        low_unit(img, layer, 0, 2)
                        dve.wait_ge(mix_high, img * 5 + 1)
                        nc.vector.tensor_tensor(main_w[0][:, 1, 0].rearrange("p t m -> p (t m)"), mixed_w[:, 0:NT[0]],
                                                main_w[0][:, 0, 0].rearrange("p t m -> p (t m)"), ALU.subtract).then_inc(mix_low, 1)
                        dve.wait_ge(mix_high, img * 5 + 2)
                        nc.vector.tensor_tensor(halo_w[0][:, 1, 0], mixed_w[:, NT[0]:E_COLS], halo_w[0][:, 0, 0],
                                                ALU.subtract).then_inc(mix_low, 1)
                        for rho in range(1, BLOCKS):
                            dve.wait_ge(mix_high, img * 5 + 2 + rho)
                            nc.vector.tensor_tensor(main_w[0][:, 1, rho].rearrange("p t m -> p (t m)"), psum[:, 1, rho - 1, 0:NT[0]],
                                                    main_w[0][:, 0, rho].rearrange("p t m -> p (t m)"), ALU.subtract).then_inc(mix_low, 1)
                    else:
                        if layer < 3:
                            dve.wait_ge(high_done, half_no(img, layer, 0, 0))
                            nc.vector.tensor_tensor(wrap[3 * Q:4 * Q, 1, PAD:PAD + W], normed[3 * Q:4 * Q, 0, 0, :],
                                                    wrap[3 * Q:4 * Q, 0, PAD:PAD + W], ALU.subtract).then_inc(low_done, 1)
                        for k in range(3):
                            low_unit(img, layer, 0, k)
                    def four_units(i, first):
                        for k in range(4):
                            low_unit(img, layer, *((i, 3) if k == 0 else (i + 1, k - 1)))
                            output_unit(img, layer, i, k)
                            if layer == 3 and (k >= 2 or not first):
                                next_statistics(img, *((i, k - 2) if k >= 2 else (i - 1, k + 2)))

                    four_units(0, True)
                    with dve.Fori(1, 3) as i:
                        four_units(i, False)
                    for k in range(4):
                        if k == 0:
                            low_unit(img, layer, 3, 3)
                        output_unit(img, layer, 3, k)
                        if layer == 3:
                            next_statistics(img, *divmod(12 + k - 2, 4))
                    if layer == 3:
                        next_statistics(img, 3, 2)
                        next_statistics(img, 3, 3)
                assert done[0] == STEPS_ALL, done

        @block.tensor
        def _(pe):
            def conv_unit(img, layer, i, k, first):
                if not first:
                    pe.wait_ge(y_done, unit_no(img, layer, i * 4 + k - 1))
                pe.wait_ge(split_done, half_no(img, layer, i * 4 + k, 2))
                into, taps, w = psum[:, k % 2, :, :], TAPS[layer], main_w[layer]
                for rho in range(BLOCKS):
                    for t in range(taps):
                        at = PAD + t - taps // 2
                        for w_part, x_part in ((0, 0), (0, 1), (1, 0)):
                            nc.tensor.matmul(into[:, rho, :], w[:, w_part, rho, t, :], split[:, k, rho, x_part, at:at + W],
                                             start=(t == 0 and w_part == 0 and x_part == 0), stop=False, skip_group_check=True)
                pe.wait_ge(halo_in[k], halo_level(img, layer, k, i))
                for w_part, x_part in ((0, 0), (0, 1), (1, 0)):
                    for pair in range(1 + (layer == 3)):
                        for rho in range(BLOCKS):
                            q = Q * ((rho + pair) % 4)
                            last = nc.tensor.matmul(into[q:q + Q, rho, :], halo_w[layer][:, w_part, pair, :],
                                                    halo[:, k % 2, rho, x_part, 0:W], start=False, stop=(w_part == 1),
                                                    tile_position=(0, q), skip_group_check=True)
                last.then_inc(conv_done, 1)

            pe.wait_ge(filled, 2)
            pe.wait_ge(consts_in, 3 * DMA)
            pe.wait_ge(fixed_low, 6)
            with pe.Fori(0, N_IMG) as img:
                for layer in range(LAYERS):
                    pe.wait_ge(agg_done, img * LAYERS + layer + 1)
                    nc.tensor.matmul(mean_ps, group_avg[:, :], agg[:, 0:1], start=True, stop=True).then_inc(mean_done, 1)
                    pe.wait_ge(var_p_done, img * LAYERS + layer + 1)
                    nc.tensor.matmul(var_ps, group_avg[:, :], var_p[:, :], start=True, stop=True).then_inc(var_done, 1)
                    if layer == 0:
                        pe.wait_ge(zed_done, img + 1)
                        nc.tensor.matmul(logit_ps, ones[:, :], zed[:, :], start=True, stop=True).then_inc(logit_done, 1)
                        pe.wait_ge(mixed_done, img + 1)
                        mixed = mixed_w[:, 0:NT[0]].rearrange("p (t m) -> p t m", t=TAPS[0])
                        for rho in range(1, BLOCKS):
                            turned = psum[:, 1, rho - 1, 0:NT[0]].rearrange("p (t m) -> p t m", t=TAPS[0])
                            nc.tensor.matmul(turned[:, :, Q * rho:P], turns[:, rho - 1, :], mixed[:, :, 0:P - Q * rho],
                                             start=True, stop=True, skip_group_check=True)
                            nc.tensor.matmul(turned[:, :, 0:Q * rho], turns[:, rho - 1, :], mixed[:, :, P - Q * rho:P],
                                             start=True, stop=True, skip_group_check=True).then_inc(turned_done, 1)
                        pe.wait_ge(mix_low, img * 5 + 5)
                    pe.wait_ge(scalars_done, img * LAYERS + layer + 1)
                    for k in range(4):
                        conv_unit(img, layer, 0, k, k < 2)
                    with pe.Fori(1, 4) as i:
                        for k in range(4):
                            conv_unit(img, layer, i, k, False)


def lay_out(L0_conv_w_experts, L0_conv_bias, L0_conv_fc_w, L0_conv_fc_b, L1_conv_weight, L2_conv_weight, L3_conv_filter_w):
    import numpy as np

    def banded(w, rho):
        m = np.zeros((P, 3, P), np.float32)
        for ro in range(ROWS):
            for kh in range(3):
                ri = ro + kh - 1
                if 0 <= ri < ROWS:
                    a, b = row_partition(ri, rho), row_partition(ro, rho)
                    m[a:a + C, :, b:b + C] = w[:, :, kh, :].transpose(1, 2, 0)
        return m

    def halo_banded(w):
        m = np.zeros((P, Q), np.float32)
        for t in range(3):
            m[Q * t:Q * t + C, 0:C] = w[:, :, 0, t].T
            m[Q * t + C:Q * t + Q, C:Q] = w[:, :, 2, t].T
        return m

    def diagonal(f, rho):
        m = np.zeros((P, 5, P), np.float32)
        for ro in range(ROWS):
            for t in range(5):
                ri = ro + t - 2
                if 0 <= ri < ROWS:
                    a, b = row_partition(ri, rho), row_partition(ro, rho)
                    m[a:a + C, t, b:b + C] = f[:, :, t].T
        return m

    def halo_diagonal(f):
        m = np.zeros((P, 2, Q), np.float32)
        outs = [(0, 0), (0, 0), (0, 1), (0, 1), (1, 0), (1, 1)]
        for n, ((_, shift), (pair, second)) in enumerate(zip(DIAGONAL_PIECES, outs)):
            m[C * n:C * n + C, pair, C * second:C * second + C] = f[:, :, shift + 2].T
        return m

    experts = np.zeros((P, EXPERTS, 3 * P + Q), np.float32)
    for e in range(EXPERTS):
        experts[:, e, 0:3 * P] = banded(L0_conv_w_experts[e], 0).reshape(P, 3 * P)
        experts[:, e, 3 * P:] = halo_banded(L0_conv_w_experts[e])
    parts = []
    for w in (L1_conv_weight, L2_conv_weight):
        w = w[:, :, ::-1, ::-1]
        parts += [banded(w, rho).reshape(P, 3 * P) for rho in range(BLOCKS)] + [halo_banded(w)]
    parts += [diagonal(L3_conv_filter_w, rho).reshape(P, 5 * P) for rho in range(BLOCKS)]
    parts += [halo_diagonal(L3_conv_filter_w).reshape(P, 2 * Q)]
    bands = np.ascontiguousarray(np.concatenate(parts, axis=1))

    consts = np.zeros((P, 4 * P), np.float32)
    partition = np.arange(P)
    group = (partition % C) // 2
    consts[:, 0:P] = np.where(group[:, None] == group[None, :], np.float32(1.0 / (P // (C // 2))), np.float32(0.0))
    for t in range(1, 4):
        consts[partition, t * P + (partition + Q * t) % P] = 1.0
    small = np.zeros((P, 2 * EXPERTS + 1), np.float32)
    for r in range(ROWS):
        small[C * r:C * r + C, 0:EXPERTS] = L0_conv_fc_w.T
        small[C * r:C * r + C, EXPERTS:2 * EXPERTS] = L0_conv_fc_b
        small[C * r:C * r + C, 2 * EXPERTS] = L0_conv_bias
    return experts, bands, consts, small


def kernel(x, L0_conv_w_experts, L0_conv_bias, L0_conv_fc_w, L0_conv_fc_b, L1_conv_weight, L2_conv_weight, L3_conv_filter_w):
    import numpy as np
    import concourse.bacc as bacc
    from concourse.bass_utils import run_bass_kernel_spmd

    weights = [np.asarray(a) for a in (L0_conv_w_experts, L0_conv_bias, L0_conv_fc_w, L0_conv_fc_b,
                                       L1_conv_weight, L2_conv_weight, L3_conv_filter_w)]
    experts, bands, consts, small = lay_out(*weights)
    arrays = {"x": np.ascontiguousarray(x), "experts": experts, "bands": bands, "consts": consts, "small": small}
    nc = bacc.Bacc("TRN2", target_bir_lowering=False, num_devices=1, dynamic_dma_scratch_size=1024)
    aps = [nc.dram_tensor(n, a.shape, mybir.dt.from_np(a.dtype), kind="ExternalInput").ap() for n, a in arrays.items()]
    out = nc.dram_tensor("out", (N_IMG, C, H, W), mybir.dt.float32, kind="ExternalOutput").ap()
    build(nc, *aps, out)
    result = run_bass_kernel_spmd(nc, [arrays], core_ids=[0])
    return result.results[0]["out"]
```

```python
import concourse.bass as bass
from concourse import mybir
from contextlib import ExitStack

N_IMG, C, H, W = 8, 16, 512, 512
P = 128
ROWS = P // C
BLOCKS = 4
UNITS = H // (ROWS * BLOCKS)
Q = 32
LAYERS = 4
PAD = 2
WP = W + 2 * PAD
SLOTS = 4
HALF = BLOCKS // 2
TAPS = 3
EXPERTS = 3
GROUP_EPS = 1e-5
SPLIT_SCALE = 64.0
SQUARE_COLS = 3 * TAPS * Q
DIAGONAL_COLS = 2 * TAPS * Q
OUTER, INNER = (0, 3), (1, 2)
SQUARE_PIECES = [(0, -1, 1, 0), (0, 0, 3, C), (1, 5, 3, 0), (1, 8, 1, 3 * C)]
DIAGONAL_PIECES = [(0, 0, -1), (0, 1, 0), (0, 2, 1), (0, 3, 2), (1, 0, 1), (1, 1, 2), (1, 2, 3), (1, 3, 4)]


def build(nc, x, experts, bands, averages, small, out):
    fp32, fp16 = mybir.dt.float32, mybir.dt.float16
    ALU, ACT, AX = mybir.AluOpType, mybir.ActivationFunctionType, mybir.AxisListType
    EXTRA = [0, 1, 1, 0]
    STEPS = [2 * UNITS + n for n in EXTRA]
    W_COLS = [SQUARE_COLS, SQUARE_COLS, SQUARE_COLS, DIAGONAL_COLS]
    DMA = 16

    ctx = ExitStack()
    with ctx:
        def sb(name, shape, dt):
            return ctx.enter_context(nc.sbuf_tensor(name, shape, dt))

        def sem(name):
            return ctx.enter_context(nc.semaphore(name))

        image = sb("image", [P, UNITS, BLOCKS, W], fp32)
        split = sb("split", [P, SLOTS, BLOCKS, 2, WP], fp16)
        windows = sb("windows", [P, 2, BLOCKS, 4, WP], fp16)
        normed = sb("normed", [P, 2, HALF, W], fp32)
        wrap = sb("wrap", [P, 2, WP], fp16)
        weights = [sb(f"weights{l}", [P, 2, W_COLS[l]], fp16) for l in range(LAYERS)]
        expert_w = sb("expert_w", [P, EXPERTS, SQUARE_COLS], fp32)
        mixed_w = sb("mixed_w", [P, SQUARE_COLS], fp32)
        stats = sb("stats", [P, UNITS, BLOCKS, 6], fp32)
        group_avg = sb("group_avg_sb", [P, P], fp32)
        ones = sb("ones", [P, P], fp32)
        tiny = sb("tiny", [P, 2 * EXPERTS + 1], fp32)
        agg = sb("agg", [P, 2], fp32)
        mean = sb("mean", [P, 1], fp32)
        dev = sb("dev", [P, 1], fp32)
        var_p = sb("var_p", [P, 1], fp32)
        var_eps = sb("var_eps", [P, 1], fp32)
        minus_half = sb("minus_half", [P, 1], fp32)
        root = sb("root", [P, 1], fp32)
        newton = sb("newton", [P, 2], fp32)
        scale = sb("scale", [P, 1], fp32)
        shift = sb("shift", [P, 1], fp32)
        zed = sb("zed", [P, EXPERTS], fp32)
        logits = sb("logits", [P, EXPERTS], fp32)
        top = sb("top", [P, 2], fp32)
        expd = sb("expd", [P, EXPERTS], fp32)
        total = sb("total", [P, 2], fp32)
        routing = sb("routing", [P, EXPERTS], fp32)
        psum = ctx.enter_context(nc.psum_tensor("psum", [P, 2, BLOCKS, W], fp32))

        fc_w, fc_b, bias = tiny[:, 0:EXPERTS], tiny[:, EXPERTS:2 * EXPERTS], tiny[:, 2 * EXPERTS:2 * EXPERTS + 1]
        mean_ps, var_ps, logit_ps = psum[:, 0, 0, 0:1], psum[:, 0, 1, 0:1], psum[:, 0, 2, 0:EXPERTS]
        stage = image[:, UNITS - 1, :, :].rearrange("p b w -> p (b w)")

        x_in = [sem(f"x_in{k}") for k in range(4)]
        x_out = [sem(f"x_out{k}") for k in range(4)]
        windows_in = [sem(f"windows_in{k}") for k in range(4)]
        row0_in = sem("row0_in")
        consts_in = sem("consts_in")
        bands_in = sem("bands_in")
        fixed_high = sem("fixed_high")
        fixed_low = sem("fixed_low")
        filled = sem("filled")
        high_done = sem("high_done")
        low_done = sem("low_done")
        split_done = sem("split_done")
        bias_done = sem("bias_done")
        conv_done = sem("conv_done")
        y_done = sem("y_done")
        stats_done = sem("stats_done")
        agg_done = sem("agg_done")
        mean_done = sem("mean_done")
        var_p_done = sem("var_p_done")
        var_done = sem("var_done")
        var_eps_done = sem("var_eps_done")
        root_done = sem("root_done")
        scalars_done = sem("scalars_done")
        zed_done = sem("zed_done")
        logit_done = sem("logit_done")
        top_done = sem("top_done")
        exp_done = sem("exp_done")
        mixed_done = sem("mixed_done")
        mix_high = sem("mix_high")
        mix_low = sem("mix_low")
        dve_step = sem("dve_step")

        block = ctx.enter_context(nc.Block())

        def halves(img, layer, i, k, h):
            return img * (2 * LAYERS * UNITS) + i * 8 + (2 * layer * UNITS + 2 * k + h)

        def step_in_layer(layer, i, k, h):
            first_unit = isinstance(i, int) and i == 0 and k == 0
            return 2 * k + h + (0 if first_unit else EXTRA[layer])

        def step(img, layer, i, k, h):
            return img * sum(STEPS) + i * 8 + (sum(STEPS[:layer]) + step_in_layer(layer, i, k, h) + 1)

        def edge_step(img, layer):
            return img * sum(STEPS) + (sum(STEPS[:layer]) + 3)

        def window_dmas(layer, k):
            pieces, split_ones = (16 // 2, 2) if layer < 3 else (len(DIAGONAL_PIECES), 1)
            return pieces + (split_ones if k in (0, 3) else 0)

        def windows_level(img, layer, i, k):
            in_image = sum(4 * window_dmas(l, k) for l in range(LAYERS))
            before = sum(4 * window_dmas(l, k) for l in range(layer))
            return img * (DMA * in_image) + i * (DMA * window_dmas(layer, k)) + DMA * (before + window_dmas(layer, k))

        def x_level(img, i):
            return img * (4 * BLOCKS * DMA) + (i * (BLOCKS * DMA) + BLOCKS * DMA)

        def dram_rows(t, img, i, k, b):
            v = t[bass.ds(img, 1)].rearrange("o c (i k b r) w -> (o r) c i k b w", k=4, b=BLOCKS, r=ROWS)
            return v[:, :, bass.ds(i, 1), k, b, :]

        def image_block(i, k, b):
            return image[:, :, :, :].rearrange("p (i k) b w -> p i k b w", k=4)[:, bass.ds(i, 1), k, b, :]

        def image_half(i, k, h, n=HALF):
            v = image[:, :, :, :].rearrange("p u b w -> p (u b) w")
            return v[:, bass.ds(i * (4 * BLOCKS) + (k * BLOCKS + h * HALF), n), :]

        @block.sync
        def _(sp):
            def load_unit(img, i, k):
                for b in range(BLOCKS):
                    sp.dma_start(image_block(i, k, b), dram_rows(x, img, i, k, b)).then_inc(x_in[k], DMA)

            def store_unit(img, i, k):
                for b in range(BLOCKS):
                    sp.dma_start(dram_rows(out, img, i, k, b), image_block(i, k, b)).then_inc(x_out[k], DMA)

            def runs(t, first, n, start, step_size, count, length):
                a = t[first:first + n]
                return bass.AP(a.tensor, a.offset + start, [[a.ap[0][0], n], [step_size, count], [1, length]])

            def sources(layer, u, k, side, first, row):
                at = lambda slot, b: (slot % SLOTS * BLOCKS + b) * (2 * WP)
                if side == 0:
                    return [(0, BLOCKS, split, first, at(k, 0))]
                if side < 0:
                    inside = (1, BLOCKS - 1, split, first, at(k, 0))
                    if k > 0:
                        return [(0, BLOCKS, split, first, at(k, 0) - 2 * WP)]
                    if u > 0:
                        return [(0, 1, split, first, at(SLOTS - 1, BLOCKS - 1)), inside]
                    if layer == 0:
                        return [(0, 1, split, C, at(k, 0)), inside]
                    return [(0, 1, wrap, 7 * C if layer < 3 else Q, 0), inside]
                inside = (0, BLOCKS - 1, split, first, at(k, 1))
                if k < 3:
                    return [(0, BLOCKS, split, first, at(k, 1))]
                if u < UNITS - 1:
                    return [inside, (BLOCKS - 1, 1, split, first, at(0, 0))]
                if layer == 0:
                    return [inside, (BLOCKS - 1, 1, split, 6 * C, at(k, BLOCKS - 1))]
                return [inside, (BLOCKS - 1, 1, wrap, 0 if layer < 3 else Q, 0)]

            def fetch_windows(layer, u, k):
                n_dmas, slot = 0, k % 2 * BLOCKS * 4 * WP
                if layer < 3:
                    for window, row, n_rows, into in SQUARE_PIECES:
                        side = row // ROWS
                        for part in range(2):
                            for b, n, t, first, at in sources(layer, u, k, side, row % ROWS * C, row):
                                sp.dma_start(runs(windows, into + part * 4 * C, n_rows * C, slot + (b * 4 + window) * WP, 4 * WP, n, WP),
                                             runs(t, first, n_rows * C, at + part * WP, 2 * WP, n, WP)).then_inc(windows_in[k], DMA)
                                n_dmas += 1
                else:
                    for window, g, quadrant in DIAGONAL_PIECES:
                        skew = 2 * (g - 1) - 3
                        c0 = max(0, -PAD - skew)
                        c1 = min(WP, W + PAD - skew)
                        for b, n, t, first, at in sources(layer, u, k, quadrant // 4, quadrant % 4 * Q, None):
                            sp.dma_start(runs(windows, g * Q, Q, slot + (b * 4 + window * 2) * WP + c0, 4 * WP, n, WP + c1 - c0),
                                         runs(t, first, Q, at + c0 + skew + PAD, 2 * WP, n, WP + c1 - c0)).then_inc(windows_in[k], DMA)
                            n_dmas += 1
                assert n_dmas == window_dmas(layer, k)

            def windows_step(img, layer, i, k, u):
                if u >= 2:
                    level = sp.to_reg(halves(img, layer, i, k - 1, 0))
                    sp.wait_ge(bands_in, DMA)
                    sp.wait_ge(conv_done, level)
                level = sp.to_reg(step(img, layer, i, k + 1, 0) if u < UNITS - 1 else step(img, layer, i, k, 1))
                sp.wait_ge(bands_in, DMA)
                sp.wait_ge(split_done, level)
                fetch_windows(layer, u, k)

            def store_step(img, i, k):
                level = sp.to_reg(halves(img, 3, i, k, 2))
                sp.wait_ge(bands_in, DMA)
                sp.wait_ge(y_done, level)
                store_unit(img, i, k)

            def reload_step(img, i, k):
                with sp.If(img < N_IMG - 1):
                    level = sp.to_reg(x_level(img, i))
                    sp.wait_ge(bands_in, DMA)
                    sp.wait_ge(x_out[k], level)
                    level = sp.to_reg(x_level(img, i + 3))
                    sp.wait_ge(bands_in, DMA)
                    sp.wait_ge(x_in[k], level)
                    load_unit(nc.s_assert_within(img + 1, 1, N_IMG - 1, skip_runtime_bounds_check_because="only images before the last come here"), i, k)

            sp.dma_start(stage[:, 0:sum(W_COLS[1:])], bands).then_inc(bands_in, DMA)
            for u in range(UNITS):
                i, k = divmod(u, 4)
                if u >= 4:
                    sp.wait_ge(x_in[k], x_level(0, i - 1))
                if u == UNITS - 1:
                    sp.wait_ge(fixed_low, 3)
                load_unit(0, i, k)
                if u == 3:
                    sp.dma_start(group_avg[:, :], averages).then_inc(consts_in, DMA)
                    sp.dma_start(tiny[:, :], small).then_inc(consts_in, DMA)
                    sp.dma_start(expert_w[:, :, :], experts).then_inc(consts_in, DMA)
            sp.wait_ge(filled, 1)

            with sp.Fori(0, N_IMG) as img:
                for layer in range(3):
                    windows_step(img, layer, 0, 0, 0)
                    if layer > 0:
                        sp.dma_start(wrap[0:C, :, :], split[0:C, 0, 0, :, :]).then_inc(row0_in, DMA)
                        level = sp.to_reg(img * (2 * DMA) + layer * DMA)
                        sp.wait_ge(bands_in, DMA)
                        sp.wait_ge(row0_in, level)
                    for u in range(1, 4):
                        windows_step(img, layer, 0, u, u)
                    with sp.Fori(1, 3) as i:
                        for k in range(4):
                            windows_step(img, layer, i, k, 4 + k)
                    for u in range(12, UNITS):
                        windows_step(img, layer, 3, u % 4, u)
                for u in range(4):
                    windows_step(img, 3, 0, u, u)
                    if u >= 2:
                        store_step(img, 0, u - 2)
                    if u >= 3:
                        reload_step(img, 0, u - 3)
                with sp.Fori(1, 3) as i:
                    for k in range(4):
                        windows_step(img, 3, i, k, 4 + k)
                        store_step(img, *((i, k - 2) if k >= 2 else (i - 1, k + 2)))
                        reload_step(img, *((i, k - 3) if k >= 3 else (i - 1, k + 1)))
                for u in range(12, UNITS + 2):
                    if u < UNITS:
                        windows_step(img, 3, 3, u % 4, u)
                    store_step(img, *divmod(u - 2, 4))
                    reload_step(img, *divmod(u - 3, 4))
                reload_step(img, *divmod(UNITS - 1, 4))
            for k in range(4):
                sp.wait_ge(x_out[k], x_level(N_IMG - 1, 3))

        @block.gpsimd
        def _(pool):
            def pad_columns(layer, t):
                def col(w, n=1):
                    return t[..., PAD + w:PAD + w + n] if len(t.shape) == 3 else t[:, :, :, PAD + w:PAD + w + n]
                if layer == 3:
                    nc.gpsimd.memset(col(-2, 2), 0.0)
                    return nc.gpsimd.memset(col(W, 2), 0.0)
                left, right = (1, W - 2) if layer == 0 else (W - 1, 0)
                nc.gpsimd.tensor_copy(col(-1), col(left))
                return nc.gpsimd.tensor_copy(col(W), col(right))

            def pad_half(img, layer, i, k, h):
                level = pool.to_reg(step(img, layer, i, k, h))
                pool.wait_ge(filled, 1)
                pool.wait_ge(low_done, level)
                pad_columns(layer, split[:, k, HALF * h:HALF * h + HALF, :, :]).then_inc(split_done, 1)

            nc.gpsimd.memset(wrap[:, :, :], 0.0)
            nc.gpsimd.memset(windows[:, :, :, :, :], 0.0)
            for col in (0, WP - PAD):
                nc.gpsimd.memset(split[:, :, :, :, col:col + PAD], 0.0)
            nc.gpsimd.memset(ones[:, :], 1.0)
            nc.gpsimd.memset(minus_half[:, :], -0.5).then_inc(filled, 1)
            pool.wait_ge(filled, 1)

            with pool.Fori(0, N_IMG) as img:
                for layer in range(LAYERS):
                    pool.wait_ge(var_eps_done, img * LAYERS + layer + 1)
                    nc.gpsimd.tensor_tensor(root[:, :], var_eps[:, :], minus_half[:, :], ALU.pow).then_inc(root_done, 1)
                    for h in range(2):
                        pad_half(img, layer, 0, 0, h)
                    if EXTRA[layer]:
                        level = pool.to_reg(edge_step(img, layer))
                        pool.wait_ge(filled, 1)
                        pool.wait_ge(low_done, level)
                        pad_columns(layer, wrap[:, :, :]).then_inc(split_done, 1)
                    for k in range(1, 4):
                        for h in range(2):
                            pad_half(img, layer, 0, k, h)
                    with pool.Fori(1, 4) as i:
                        for k in range(4):
                            for h in range(2):
                                pad_half(img, layer, i, k, h)

        @block.scalar
        def _(act):
            def normalize(into, source, partitions=slice(0, P)):
                return nc.scalar.activation(into, source, ACT.Identity, bias=shift[partitions, :], scale=scale[partitions, :])

            def high_half(img, layer, i, k, h):
                n = step_in_layer(layer, i, k, h)
                if not (isinstance(i, int) and i == 0 and n < 2):
                    act.wait_ge(low_done, step(img, layer, i, k, h) - 2)
                source = image_half(i, k, h)
                normalize(normed[:, n % 2, :, :], source)
                normalize(split[:, k, HALF * h:HALF * h + HALF, 0, PAD:PAD + W], source).then_inc(high_done, 1)

            def high_unit(img, layer, i, k, wait_slot):
                if wait_slot:
                    act.wait_ge(conv_done, halves(img, layer, i - 1, k, 2))
                    act.wait_ge(windows_in[(k + 1) % 4], windows_level(img, layer, i - 1 if k < 3 else i, (k + 1) % 4))
                for h in range(2):
                    high_half(img, layer, i, k, h)
                if layer == 0:
                    level = act.to_reg(step(img, layer, i, k, 1))
                    act.wait_ge(bands_in, DMA)
                    act.wait_ge(high_done, level)
                    whole = image_half(i, k, 0, BLOCKS)
                    nc.scalar.activation(whole, whole, ACT.Identity, bias=bias, scale=1.0).then_inc(bias_done, 1)

            act.wait_ge(bands_in, DMA)
            at = 0
            for layer in (1, 2, 3):
                nc.scalar.activation(weights[layer][:, 0, :], stage[:, at:at + W_COLS[layer]], ACT.Copy,
                                     scale=SPLIT_SCALE).then_inc(fixed_high, 1)
                at += W_COLS[layer]

            with act.Fori(0, N_IMG) as img:
                for layer in range(LAYERS):
                    act.wait_ge(scalars_done, img * LAYERS + layer + 1)
                    for k in range(4):
                        high_unit(img, layer, 0, k, False)
                        if layer == 0 and k == 0:
                            act.wait_ge(top_done, img + 1)
                            nc.scalar.activation(expd[:, :], logits[:, :], ACT.Exp, bias=top[:, 1:2], scale=1.0,
                                                 accum_out=total[:, 0:1]).then_inc(exp_done, 1)
                            act.wait_ge(mixed_done, img + 1)
                            nc.scalar.copy(weights[0][:, 0, :], mixed_w[:, :]).then_inc(mix_high, 1)
                        if EXTRA[layer] and k == 0:
                            edge = slice(3 * Q, 4 * Q)
                            source = image[edge, UNITS - 1, BLOCKS - 1, :]
                            act.wait_ge(low_done, edge_step(img, layer) - 2)
                            normalize(normed[edge, 0, 0, :], source, edge)
                            normalize(wrap[edge, 0, PAD:PAD + W], source, edge).then_inc(high_done, 1)
                    with act.Fori(1, 4) as i:
                        for k in range(4):
                            high_unit(img, layer, i, k, True)

        @block.vector
        def _(dve):
            SMALL_STEPS = 4 * LAYERS + 6

            def low_half(img, layer, i, k, h):
                n = step_in_layer(layer, i, k, h) % 2
                dve.wait_ge(high_done, step(img, layer, i, k, h))
                nc.vector.tensor_tensor(split[:, k, HALF * h:HALF * h + HALF, 1, PAD:PAD + W], normed[:, n, :, :],
                                        split[:, k, HALF * h:HALF * h + HALF, 0, PAD:PAD + W],
                                        ALU.subtract).then_inc(low_done, 1)

            def low_unit(img, layer, i, k):
                low_half(img, layer, i, k, 0)
                low_half(img, layer, i, k, 1)

            def statistics(i, k, h):
                v = stats[:, :, :, :].rearrange("p u b s -> p (u b) s")
                for b in range(HALF):
                    block_no = i * (4 * BLOCKS) + (k * BLOCKS + h * HALF + b)
                    last = nc.vector.bn_stats(v[:, bass.ds(block_no, 1), :].rearrange("p o s -> p (o s)"),
                                              image[:, :, :, :].rearrange("p u b w -> p (u b) w")[:, bass.ds(block_no, 1), :].rearrange("p o w -> p (o w)"))
                last.then_inc(stats_done, 1)

            def output_unit(img, layer, i, k):
                for h in range(2):
                    dve.wait_ge(conv_done, halves(img, layer, i, k, h + 1))
                    if layer == 0:
                        dve.wait_ge(bias_done, img * UNITS + i * 4 + (k + 1))
                    x_half = image_half(i, k, h)
                    nc.vector.scalar_tensor_tensor(x_half, psum[:, k % 2, HALF * h:HALF * h + HALF, :], 1.0 / SPLIT_SCALE ** 2,
                                                   x_half, ALU.mult, ALU.add).then_inc(y_done, 1)
                    if layer < 3:
                        dve.wait_ge(y_done, halves(img, layer, i, k, h + 1))
                        statistics(i, k, h)

            def next_statistics(img, i, k):
                with dve.If(img < N_IMG - 1):
                    dve.wait_ge(x_in[k], x_level(img, i + 4))
                    statistics(i, k, 0)
                    statistics(i, k, 1)

            at = 0
            for layer in (1, 2, 3):
                dve.wait_ge(fixed_high, layer)
                nc.vector.scalar_tensor_tensor(weights[layer][:, 1, :], stage[:, at:at + W_COLS[layer]], SPLIT_SCALE,
                                               weights[layer][:, 0, :], ALU.mult, ALU.subtract).then_inc(fixed_low, 1)
                at += W_COLS[layer]
            for u in range(UNITS):
                i, k = divmod(u, 4)
                dve.wait_ge(x_in[k], x_level(0, i))
                statistics(i, k, 0)
                statistics(i, k, 1)
            dve.wait_ge(consts_in, 3 * DMA)

            with dve.Fori(0, N_IMG) as img:
                done = [0]

                def small(instruction):
                    done[0] += 1
                    instruction.then_inc(dve_step, 1)
                    dve.wait_ge(dve_step, img * SMALL_STEPS + done[0])

                for layer in range(LAYERS):
                    level = dve.to_reg(halves(img, layer, 4, 0, 0))
                    dve.wait_ge(consts_in, 3 * DMA)
                    dve.wait_ge(stats_done, level)
                    nc.vector.bn_aggr(agg[:, :], stats[:, :, :, :].rearrange("p u b s -> p (u b s)")).then_inc(agg_done, 1)
                    dve.wait_ge(mean_done, img * LAYERS + layer + 1)
                    nc.vector.tensor_copy(mean[:, :], mean_ps)
                    small(nc.vector.tensor_tensor(dev[:, :], agg[:, 0:1], mean_ps, ALU.subtract))
                    nc.vector.scalar_tensor_tensor(var_p[:, :], dev[:, :], dev[:, :], agg[:, 1:2],
                                                   ALU.mult, ALU.add).then_inc(var_p_done, 1)
                    dve.wait_ge(var_done, img * LAYERS + layer + 1)
                    nc.vector.tensor_scalar(var_eps[:, :], var_ps, GROUP_EPS, None, ALU.add).then_inc(var_eps_done, 1)
                    dve.wait_ge(root_done, img * LAYERS + layer + 1)
                    small(nc.vector.scalar_tensor_tensor(newton[:, 0:1], root[:, :], var_eps[:, :], root[:, :],
                                                         ALU.mult, ALU.mult))
                    small(nc.vector.tensor_scalar(newton[:, 1:2], newton[:, 0:1], -0.5, 1.5, ALU.mult, ALU.add))
                    small(nc.vector.scalar_tensor_tensor(scale[:, :], root[:, :], SPLIT_SCALE, newton[:, 1:2],
                                                         ALU.mult, ALU.mult))
                    nc.vector.scalar_tensor_tensor(shift[:, :], mean[:, :], -1.0, scale[:, :],
                                                   ALU.mult, ALU.mult).then_inc(scalars_done, 1)
                    if layer == 0:
                        nc.vector.tensor_scalar(zed[:, :], fc_w, dev[:, :], scale[:, :], ALU.mult, ALU.mult).then_inc(zed_done, 1)
                        dve.wait_ge(logit_done, img + 1)
                        small(nc.vector.scalar_tensor_tensor(logits[:, :], logit_ps, 1.0 / (SPLIT_SCALE * ROWS), fc_b,
                                                             ALU.mult, ALU.add))
                        small(nc.vector.reduce_max(top[:, 0:1], logits[:, :], AX.X))
                        nc.vector.tensor_scalar(top[:, 1:2], top[:, 0:1], -1.0, None, ALU.mult).then_inc(top_done, 1)
                        low_unit(img, layer, 0, 0)
                        dve.wait_ge(exp_done, img + 1)
                        small(nc.vector.reciprocal(total[:, 1:2], total[:, 0:1]))
                        small(nc.vector.tensor_scalar(routing[:, :], expd[:, :], total[:, 1:2], SPLIT_SCALE, ALU.mult, ALU.mult))
                        small(nc.vector.tensor_scalar(mixed_w[:, :], expert_w[:, 0, :], routing[:, 0:1], None, ALU.mult))
                        small(nc.vector.scalar_tensor_tensor(mixed_w[:, :], expert_w[:, 1, :], routing[:, 1:2], mixed_w[:, :],
                                                             ALU.mult, ALU.add))
                        nc.vector.scalar_tensor_tensor(mixed_w[:, :], expert_w[:, 2, :], routing[:, 2:3], mixed_w[:, :],
                                                       ALU.mult, ALU.add).then_inc(mixed_done, 1)
                        dve.wait_ge(mix_high, img + 1)
                        nc.vector.tensor_tensor(weights[0][:, 1, :], mixed_w[:, :], weights[0][:, 0, :],
                                                ALU.subtract).then_inc(mix_low, 1)
                    else:
                        low_unit(img, layer, 0, 0)
                        if EXTRA[layer]:
                            edge = slice(3 * Q, 4 * Q)
                            dve.wait_ge(high_done, edge_step(img, layer))
                            nc.vector.tensor_tensor(wrap[edge, 1, PAD:PAD + W], normed[edge, 0, 0, :],
                                                    wrap[edge, 0, PAD:PAD + W], ALU.subtract).then_inc(low_done, 1)
                    low_unit(img, layer, 0, 1)
                    low_unit(img, layer, 0, 2)

                    def four_units(i, first):
                        for k in range(4):
                            low_unit(img, layer, *((i, 3) if k == 0 else (i + 1, k - 1)))
                            output_unit(img, layer, i, k)
                            if layer == 3 and (k >= 2 or not first):
                                next_statistics(img, *((i, k - 2) if k >= 2 else (i - 1, k + 2)))

                    four_units(0, True)
                    with dve.Fori(1, 3) as i:
                        four_units(i, False)
                    for k in range(4):
                        if k == 0:
                            low_unit(img, layer, 3, 3)
                        output_unit(img, layer, 3, k)
                        if layer == 3:
                            next_statistics(img, *divmod(12 + k - 2, 4))
                    if layer == 3:
                        next_statistics(img, 3, 2)
                        next_statistics(img, 3, 3)
                assert done[0] == SMALL_STEPS

        @block.tensor
        def _(pe):
            PRODUCTS = ((0, 0), (0, 1), (1, 0))

            def inner_products(layer, k, b, q):
                w = weights[layer][:, :, :].rearrange("p s (m t n) -> p s m t n", m=3, n=Q)
                return [(w[:, w_part, q, t, :], split[:, k, b, x_part, PAD + t - 1:PAD + t - 1 + W])
                        for t in range(TAPS) for w_part, x_part in PRODUCTS]

            def outer_products(layer, k, b, q):
                w = weights[layer][:, :, :].rearrange("p s (m t n) -> p s m t n", m=3, n=Q)
                return [(w[:, w_part, 0, t, :], windows[:, k % 2, b, OUTER.index(q), PAD + t - 1:PAD + t - 1 + W])
                        for t in range(TAPS) for w_part in range(2)]

            def diagonal_products(k, b, q):
                w = weights[3][:, :, :].rearrange("p s (m t n) -> p s m t n", m=2, n=Q)
                first = 3 - 2 * (q % 2)
                return [(w[:, w_part, q % 2, t, :], windows[:, k % 2, b, q // 2 * 2 + x_part, first + t - 1:first + t - 1 + W])
                        for t in range(TAPS) for w_part, x_part in PRODUCTS]

            def multiply(k, b, products):
                last = None
                for n in range(max(len(p) for p in products.values())):
                    for q, p in products.items():
                        if n < len(p):
                            last = nc.tensor.matmul(psum[Q * q:Q * q + Q, k % 2, b, :], *p[n], start=(n == 0), stop=(n == len(p) - 1),
                                                    tile_position=(0, Q * q), skip_group_check=True)
                return last

            def conv_unit(img, layer, i, k):
                first_unit = isinstance(i, int) and i == 0 and k == 0
                for h in range(2):
                    if not (isinstance(i, int) and i == 0 and k < 2):
                        pe.wait_ge(y_done, halves(img, layer, i, k - 2, h + 1))
                    if first_unit and layer < 3:
                        pe.wait_ge(split_done, step(img, layer, i, k, h))
                        for b in range(HALF * h, HALF * h + HALF):
                            multiply(k, b, {q: inner_products(layer, k, b, q) for q in INNER})
                if not first_unit and layer < 3:
                    pe.wait_ge(split_done, step(img, layer, i, k, 1))
                pe.wait_ge(windows_in[k], windows_level(img, layer, i, k))
                for h in range(2):
                    for b in range(HALF * h, HALF * h + HALF):
                        if layer == 3:
                            products = {q: diagonal_products(k, b, q) for q in range(4)}
                        else:
                            products = {q: outer_products(layer, k, b, q) for q in OUTER}
                            if not first_unit:
                                products.update({q: inner_products(layer, k, b, q) for q in INNER})
                        last = multiply(k, b, products)
                    last.then_inc(conv_done, 1)

            pe.wait_ge(filled, 1)
            pe.wait_ge(consts_in, 3 * DMA)
            pe.wait_ge(fixed_low, 3)
            with pe.Fori(0, N_IMG) as img:
                for layer in range(LAYERS):
                    pe.wait_ge(agg_done, img * LAYERS + layer + 1)
                    nc.tensor.matmul(mean_ps, group_avg[:, :], agg[:, 0:1], start=True, stop=True).then_inc(mean_done, 1)
                    pe.wait_ge(var_p_done, img * LAYERS + layer + 1)
                    nc.tensor.matmul(var_ps, group_avg[:, :], var_p[:, :], start=True, stop=True).then_inc(var_done, 1)
                    if layer == 0:
                        pe.wait_ge(zed_done, img + 1)
                        nc.tensor.matmul(logit_ps, ones[:, :], zed[:, :], start=True, stop=True).then_inc(logit_done, 1)
                        pe.wait_ge(mix_low, img + 1)
                    pe.wait_ge(scalars_done, img * LAYERS + layer + 1)
                    for k in range(4):
                        conv_unit(img, layer, 0, k)
                    with pe.Fori(1, 4) as i:
                        for k in range(4):
                            conv_unit(img, layer, i, k)


def lay_out(L0_conv_w_experts, L0_conv_bias, L0_conv_fc_w, L0_conv_fc_b, L1_conv_weight, L2_conv_weight, L3_conv_filter_w):
    import numpy as np

    def window(w):
        m = np.zeros((2, 4, C, TAPS, 2, C), np.float32)
        for out_row in range(2):
            for kh in range(3):
                m[:, out_row + kh, :, :, out_row, :] = w[:, :, kh, :].transpose(1, 2, 0)
        return m.reshape(P, TAPS * Q)

    def inner(w, q):
        m = np.zeros((ROWS, C, TAPS, 2, C), np.float32)
        for out_row in range(2):
            for kh in range(3):
                m[2 * q + out_row + kh - 1, :, :, out_row, :] = w[:, :, kh, :].transpose(1, 2, 0)
        return m.reshape(P, TAPS * Q)

    def square(w):
        return np.concatenate([window(w)] + [inner(w, q) for q in INNER], axis=1)

    def diagonal(f):
        m = np.zeros((4, 2, C, 2, TAPS, 2, C), np.float32)
        for g in range(4):
            for row in range(2):
                for place in range(2):
                    for out_row in range(2):
                        tap = 2 * (g - 1 - place) + row - out_row
                        if -2 <= tap <= 2:
                            m[g, row, :, place, row - out_row + 1, out_row, :] = f[:, :, tap + 2].T
        return m.reshape(P, DIAGONAL_COLS)

    experts = np.stack([square(w) for w in L0_conv_w_experts], axis=1)
    bands = np.concatenate([square(L1_conv_weight[:, :, ::-1, ::-1]), square(L2_conv_weight[:, :, ::-1, ::-1]),
                            diagonal(L3_conv_filter_w)], axis=1)
    partition = np.arange(P)
    group = (partition % C) // 2
    group_avg = np.where(group[:, None] == group[None, :], np.float32(1.0 / (P // (C // 2))), np.float32(0.0))
    small = np.zeros((P, 2 * EXPERTS + 1), np.float32)
    for r in range(ROWS):
        small[C * r:C * r + C, 0:EXPERTS] = L0_conv_fc_w.T
        small[C * r:C * r + C, EXPERTS:2 * EXPERTS] = L0_conv_fc_b
        small[C * r:C * r + C, 2 * EXPERTS] = L0_conv_bias
    return np.ascontiguousarray(experts), np.ascontiguousarray(bands), group_avg, small


def kernel(x, L0_conv_w_experts, L0_conv_bias, L0_conv_fc_w, L0_conv_fc_b, L1_conv_weight, L2_conv_weight, L3_conv_filter_w):
    import numpy as np
    import concourse.bacc as bacc
    from concourse.bass_utils import run_bass_kernel_spmd

    weights = [np.asarray(a) for a in (L0_conv_w_experts, L0_conv_bias, L0_conv_fc_w, L0_conv_fc_b,
                                       L1_conv_weight, L2_conv_weight, L3_conv_filter_w)]
    experts, bands, group_avg, small = lay_out(*weights)
    arrays = {"x": np.ascontiguousarray(x), "experts": experts, "bands": bands, "group_avg": group_avg, "small": small}
    nc = bacc.Bacc("TRN2", target_bir_lowering=False, num_devices=1, dynamic_dma_scratch_size=1024)
    aps = [nc.dram_tensor(n, a.shape, mybir.dt.from_np(a.dtype), kind="ExternalInput").ap() for n, a in arrays.items()]
    out = nc.dram_tensor("out", (N_IMG, C, H, W), mybir.dt.float32, kind="ExternalOutput").ap()
    build(nc, *aps, out)
    result = run_bass_kernel_spmd(nc, [arrays], core_ids=[0])
    return result.results[0]["out"]
```

```python
import concourse.bass as bass
from concourse import mybir
from contextlib import ExitStack

N_IMG, C, H, W = 8, 16, 512, 512
P = 128
ROWS = P // C
BLOCKS = 4
UNITS = H // (ROWS * BLOCKS)
Q = 32
LAYERS = 4
PAD = 2
WP = W + 2 * PAD
EARLY = 3
SLOTS = 4
HALF = BLOCKS // 2
TAPS = 3
EXPERTS = 3
SCRATCH = 4096
GROUP_EPS = 1e-5
SPLIT_SCALE = 64.0
SQUARE_COLS = 3 * TAPS * Q
DIAGONAL_TAPS = 5
WINDOW_COLS = 2 * TAPS * Q
DIAGONAL_COLS = WINDOW_COLS + 2 * DIAGONAL_TAPS * Q
WHOLE_FROM = 14
OUTER, INNER = (0, 3), (1, 2)
SQUARE_PIECES = [(0, -1, 1, 0), (0, 0, 3, C), (1, 5, 3, 0), (1, 8, 1, 3 * C)]
INNER_PIECES = [(0, 3), (1, 0)]
DIAGONAL_PIECES = [(0, 0, -1), (0, 1, 0), (0, 2, 1), (0, 3, 2), (1, 0, 1), (1, 1, 2), (1, 2, 3), (1, 3, 4)]


def build(nc, x, experts, bands, averages, small, out):
    fp32, fp16 = mybir.dt.float32, mybir.dt.float16
    ALU, ACT, AX = mybir.AluOpType, mybir.ActivationFunctionType, mybir.AxisListType
    EXTRA = [0, 1, 1, 0]
    STEPS = [2 * UNITS + n for n in EXTRA]
    W_COLS = [SQUARE_COLS, SQUARE_COLS, SQUARE_COLS, DIAGONAL_COLS]
    SMALL_STEPS = (5 + 2 * EARLY) * LAYERS + 6 + sum(EXTRA)
    DMA = 16

    ctx = ExitStack()
    with ctx:
        def sb(name, shape, dt):
            return ctx.enter_context(nc.sbuf_tensor(name, shape, dt))

        def sem(name):
            return ctx.enter_context(nc.semaphore(name))

        image = sb("image", [P, UNITS, BLOCKS, W], fp32)
        split = sb("split", [P, SLOTS, BLOCKS, 2, WP], fp16)
        windows = sb("windows", [P, 2, BLOCKS, 4, WP], fp16)
        normed = sb("normed", [P, 2, HALF, W], fp32)
        wrap = sb("wrap", [P, 2, WP], fp16)
        weights = [sb(f"weights{l}", [P, 2, W_COLS[l]], fp16) for l in range(LAYERS)]
        expert_w = sb("expert_w", [P, EXPERTS, SQUARE_COLS], fp32)
        mixed_w = sb("mixed_w", [P, SQUARE_COLS], fp32)
        stats = sb("stats", [P, UNITS, BLOCKS, 6], fp32)
        group_avg = sb("group_avg_sb", [P, P], fp32)
        ones = sb("ones", [P, P], fp32)
        tiny = sb("tiny", [P, 2 * EXPERTS + 1], fp32)
        agg = sb("agg", [P, 2], fp32)
        mean = sb("mean", [P, 1], fp32)
        dev = sb("dev", [P, 1], fp32)
        var_p = sb("var_p", [P, 1], fp32)
        var_eps = sb("var_eps", [P, 1], fp32)
        minus_half = sb("minus_half", [P, 1], fp32)
        root = sb("root", [P, 1], fp32)
        newton = sb("newton", [P, 2], fp32)
        scale = sb("scale", [P, 1], fp32)
        shift = sb("shift", [P, 1], fp32)
        zed = sb("zed", [P, EXPERTS], fp32)
        logits = sb("logits", [P, EXPERTS], fp32)
        top = sb("top", [P, 2], fp32)
        expd = sb("expd", [P, EXPERTS], fp32)
        total = sb("total", [P, 2], fp32)
        routing = sb("routing", [P, EXPERTS], fp32)
        psum = ctx.enter_context(nc.psum_tensor("psum", [P, 2, BLOCKS, W], fp32))

        fc_w, fc_b, bias = tiny[:, 0:EXPERTS], tiny[:, EXPERTS:2 * EXPERTS], tiny[:, 2 * EXPERTS:2 * EXPERTS + 1]
        mean_ps, var_ps, logit_ps = psum[:, 0, 0, 0:1], psum[:, 0, 1, 0:1], psum[:, 0, 2, 0:EXPERTS]
        waiting = [split[:, k, :, :, :].rearrange("p b s w -> p (b s w)")[:, 0:2 * BLOCKS * W].bitcast(fp32) for k in (2, 3)]
        stage = image[:, UNITS - 1, :, :].rearrange("p b w -> p (b w)")

        first_in = [sem(f"first_in{k}") for k in range(4)]
        x_in = [sem(f"x_in{k}") for k in range(4)]
        tail_in = [sem(f"unit{12 + k}_in") for k in range(4)]
        x_out = [sem(f"x_out{k}") for k in range(4)]
        moved = [sem("moved_14"), sem("moved_15")]
        windows_in = [sem(f"windows_in{k}") for k in range(4)]
        far_in = [sem(f"far_in{k}") for k in range(4)]
        row0_in = sem("row0_in")
        consts_in = sem("consts_in")
        bands_in = sem("bands_in")
        fixed_high = sem("fixed_high")
        fixed_low = sem("fixed_low")
        filled = sem("filled")
        high_done = sem("high_done")
        low_done = sem("low_done")
        split_done = sem("split_done")
        bias_done = sem("bias_done")
        conv_done = sem("conv_done")
        third_done = sem("third_done")
        y_third_done = sem("y_third_done")
        y_done = sem("y_done")
        stats_done = sem("stats_done")
        agg_done = sem("agg_done")
        mean_done = sem("mean_done")
        var_p_done = sem("var_p_done")
        var_done = sem("var_done")
        var_eps_done = sem("var_eps_done")
        root_done = sem("root_done")
        zed_done = sem("zed_done")
        logit_done = sem("logit_done")
        top_done = sem("top_done")
        exp_done = sem("exp_done")
        mixed_done = sem("mixed_done")
        mix_high = sem("mix_high")
        mix_low = sem("mix_low")
        dve_step = sem("dve_step")

        block = ctx.enter_context(nc.Block())

        def halves(img, layer, i, k, h):
            return img * (2 * LAYERS * UNITS) + i * 8 + (2 * layer * UNITS + 2 * k + h)

        def step_in_layer(layer, i, k, h):
            first_unit = isinstance(i, int) and i == 0 and k == 0
            return 2 * k + h + (0 if first_unit else EXTRA[layer])

        def step(img, layer, i, k, h):
            return img * sum(STEPS) + i * 8 + (sum(STEPS[:layer]) + step_in_layer(layer, i, k, h) + 1)

        def edge_step(img, layer):
            return img * sum(STEPS) + (sum(STEPS[:layer]) + 3)

        def scalars_step(layer):
            return 5 * (layer + 1) + sum(2 * EARLY + EXTRA[l] + (6 if l == 0 else 0) for l in range(layer))

        def far_side(layer, u, k):
            return None if layer == 3 and u > 0 else 1 if k == 3 else -1

        def far_dmas(layer, u, k):
            if far_side(layer, u, k) is None:
                return 0
            if u == 0:
                return 2
            return 4 if k in (0, 3) else 2

        def near_dmas(layer, u, k):
            return 8 + (0 if k in (1, 2) else 2 if layer < 3 else 1) - far_dmas(layer, u, k)

        def windows_level(img, layer, i, k, dmas=near_dmas):
            def up_to(l, n):
                return dmas(l, k, k) + n * dmas(l, 4 + k, k)
            in_image = sum(up_to(l, 3) for l in range(LAYERS))
            before = sum(up_to(l, 3) for l in range(layer))
            return img * (DMA * in_image) + i * (DMA * dmas(layer, 4 + k, k)) + DMA * (before + up_to(layer, 0))

        def x_level(img, i):
            return img * (4 * BLOCKS * DMA) + (i * (BLOCKS * DMA) + BLOCKS * DMA)

        def x_in_level(img, i):
            return img * (3 * BLOCKS * DMA) + (i * (BLOCKS * DMA) + BLOCKS * DMA)

        def tail_level(img):
            return img * (BLOCKS * DMA) + BLOCKS * DMA

        def dram_rows(t, img, i, k, b):
            v = t[bass.ds(img, 1)].rearrange("o c (i k b r) w -> (o r) c i k b w", k=4, b=BLOCKS, r=ROWS)
            return v[:, :, bass.ds(i, 1), k, b, :]

        def image_block(i, k, b):
            return image[:, :, :, :].rearrange("p (i k) b w -> p i k b w", k=4)[:, bass.ds(i, 1), k, b, :]

        def image_half(i, k, h, n=HALF):
            v = image[:, :, :, :].rearrange("p u b w -> p (u b) w")
            return v[:, bass.ds(i * (4 * BLOCKS) + (k * BLOCKS + h * HALF), n), :]

        def runs(t, first, n, start, step_size, count, length):
            a = t[first:first + n]
            return bass.AP(a.tensor, a.offset + start, [[a.ap[0][0], n], [step_size, count], [1, length]])

        def sources(layer, u, k, side, first):
            at = lambda slot, b: (slot % SLOTS * BLOCKS + b) * (2 * WP)
            if side == 0:
                return [(0, BLOCKS, split, first, at(k, 0))]
            if side < 0:
                inside = (1, BLOCKS - 1, split, first, at(k, 0))
                if k > 0:
                    return [(0, BLOCKS, split, first, at(k, 0) - 2 * WP)]
                if u > 0:
                    return [(0, 1, split, first, at(SLOTS - 1, BLOCKS - 1)), inside]
                if layer == 0:
                    return [(0, 1, split, C, at(k, 0)), inside]
                return [(0, 1, wrap, 7 * C if layer < 3 else Q, 0), inside]
            inside = (0, BLOCKS - 1, split, first, at(k, 1))
            if k < 3:
                return [(0, BLOCKS, split, first, at(k, 1))]
            if u < UNITS - 1:
                return [inside, (BLOCKS - 1, 1, split, first, at(0, 0))]
            if layer == 0:
                return [inside, (BLOCKS - 1, 1, split, 6 * C, at(k, BLOCKS - 1))]
            return [inside, (BLOCKS - 1, 1, wrap, 0 if layer < 3 else Q, 0)]

        def fetch_windows(engine, done, layer, u, k, side, far=False):
            slot = k % 2 * BLOCKS * 4 * WP

            def share(first):
                return [run for run in sources(layer, u, k, side, first)
                        if far == (side == far_side(layer, u, k) and (u > 0 or layer == 3 or run[1] == 1))]

            if layer < 3:
                for window, row, n_rows, into in SQUARE_PIECES:
                    if row // ROWS == side:
                        for part in range(2):
                            for b, n, t, first, at in share(row % ROWS * C):
                                engine.dma_start(runs(windows, into + part * 4 * C, n_rows * C, slot + (b * 4 + window) * WP, 4 * WP, n, WP),
                                                 runs(t, first, n_rows * C, at + part * WP, 2 * WP, n, WP)).then_inc(done, DMA)
            else:
                for window, g, quadrant in DIAGONAL_PIECES:
                    if quadrant // 4 == side:
                        skew = 2 * (g - 1) - 3
                        c0 = max(0, -PAD - skew)
                        c1 = min(WP, W + PAD - skew)
                        length = c1 - c0 + (0 if (window, g) in INNER_PIECES and u < WHOLE_FROM else WP)
                        for b, n, t, first, at in share(quadrant % 4 * Q):
                            engine.dma_start(runs(windows, g * Q, Q, slot + (b * 4 + window * 2) * WP + c0, 4 * WP, n, length),
                                             runs(t, first, Q, at + c0 + skew + PAD, 2 * WP, n, length)).then_inc(done, DMA)

        @block.sync
        def _(sp):
            def store_unit(img, i, k):
                for b in range(BLOCKS):
                    sp.dma_start(dram_rows(out, img, i, k, b), image_block(i, k, b)).then_inc(x_out[k], DMA)

            def windows_step(img, layer, i, k, u):
                if u >= 2:
                    level = sp.to_reg(halves(img, layer, i, k - 1, 0))
                    sp.wait_ge(bands_in, DMA)
                    sp.wait_ge(conv_done, level)
                level = sp.to_reg(step(img, layer, i, k, 1))
                sp.wait_ge(bands_in, DMA)
                sp.wait_ge(split_done, level)
                fetch_windows(sp, windows_in[k], layer, u, k, 0)
                fetch_windows(sp, windows_in[k], layer, u, k, -1)
                if u < UNITS - 1 and far_side(layer, u, k) != 1:
                    level = sp.to_reg(step(img, layer, i, k + 1, 0))
                    sp.wait_ge(bands_in, DMA)
                    sp.wait_ge(split_done, level)
                fetch_windows(sp, windows_in[k], layer, u, k, 1)

            def store_step(img, i, k):
                level = sp.to_reg(halves(img, 3, i, k, 2))
                sp.wait_ge(bands_in, DMA)
                sp.wait_ge(y_done, level)
                store_unit(img, i, k)

            sp.dma_start(stage[:, 0:sum(W_COLS[1:])], bands).then_inc(bands_in, DMA)
            for u in range(UNITS):
                i, k = divmod(u, 4)
                if u >= 4:
                    sp.wait_ge(first_in[k], x_level(0, i - 1))
                if u == UNITS - 1:
                    sp.wait_ge(fixed_low, 3)
                for b in range(BLOCKS):
                    sp.dma_start(image_block(i, k, b), dram_rows(x, 0, i, k, b)).then_inc(first_in[k], DMA)
                if u == 3:
                    sp.dma_start(group_avg[:, :], averages).then_inc(consts_in, DMA)
                    sp.dma_start(tiny[:, :], small).then_inc(consts_in, DMA)
                    sp.dma_start(expert_w[:, :, :], experts).then_inc(consts_in, DMA)
            sp.wait_ge(filled, 1)

            with sp.Fori(0, N_IMG) as img:
                for layer in range(3):
                    windows_step(img, layer, 0, 0, 0)
                    if layer > 0:
                        sp.dma_start(wrap[0:C, :, :], split[0:C, 0, 0, :, :]).then_inc(row0_in, DMA)
                        level = sp.to_reg(img * (2 * DMA) + layer * DMA)
                        sp.wait_ge(bands_in, DMA)
                        sp.wait_ge(row0_in, level)
                    for u in range(1, 4):
                        windows_step(img, layer, 0, u, u)
                    with sp.Fori(1, 3) as i:
                        for k in range(4):
                            windows_step(img, layer, i, k, 4 + k)
                    for u in range(12, UNITS):
                        windows_step(img, layer, 3, u % 4, u)
                for u in range(4):
                    windows_step(img, 3, 0, u, u)
                    if u >= 2:
                        store_step(img, 0, u - 2)
                with sp.Fori(1, 3) as i:
                    for k in range(4):
                        windows_step(img, 3, i, k, 4 + k)
                        store_step(img, *((i, k - 2) if k >= 2 else (i - 1, k + 2)))
                for u in range(12, UNITS + 2):
                    if u < UNITS:
                        windows_step(img, 3, 3, u % 4, u)
                    store_step(img, *divmod(u - 2, 4))
                with sp.If(img < N_IMG - 1):
                    for n, k in enumerate((2, 3)):
                        level = sp.to_reg(x_level(img, 3))
                        sp.wait_ge(bands_in, DMA)
                        sp.wait_ge(x_out[k], level)
                        level = sp.to_reg(tail_level(img))
                        sp.wait_ge(bands_in, DMA)
                        sp.wait_ge(tail_in[k], level)
                        sp.dma_start(image[:, UNITS - 2 + n, :, :].rearrange("p b w -> p (b w)"), waiting[n]).then_inc(moved[n], DMA)
            for k in range(4):
                sp.wait_ge(x_out[k], x_level(N_IMG - 1, 3))

        @block.gpsimd
        def _(pool):
            def pad_columns(layer, t):
                def col(w, n=1):
                    return t[..., PAD + w:PAD + w + n] if len(t.shape) == 3 else t[:, :, :, PAD + w:PAD + w + n]
                if layer == 3:
                    nc.gpsimd.memset(col(-2, 2), 0.0)
                    return nc.gpsimd.memset(col(W, 2), 0.0)
                left, right = (1, W - 2) if layer == 0 else (W - 1, 0)
                nc.gpsimd.tensor_copy(col(-1), col(left))
                return nc.gpsimd.tensor_copy(col(W), col(right))

            def pad_half(img, layer, i, k, h):
                level = pool.to_reg(step(img, layer, i, k, h))
                pool.wait_ge(filled, 1)
                pool.wait_ge(low_done, level)
                pad_columns(layer, split[:, k, HALF * h:HALF * h + HALF, :, :]).then_inc(split_done, 1)

            def far_step(img, layer, i, k, u):
                if u >= 2:
                    level = pool.to_reg(halves(img, layer, i, k - 1, 0))
                    pool.wait_ge(filled, 1)
                    pool.wait_ge(conv_done, level)
                if u in (1, UNITS - 1) and EXTRA[layer]:
                    level = pool.to_reg(img * (2 * DMA) + layer * DMA)
                    pool.wait_ge(filled, 1)
                    pool.wait_ge(row0_in, level)
                if u == 0 and EXTRA[layer]:
                    level = pool.to_reg(edge_step(img, layer))
                elif k == 3 and u < UNITS - 1:
                    level = pool.to_reg(step(img, layer, i, k + 1, 0))
                else:
                    level = pool.to_reg(step(img, layer, i, k, 1))
                pool.wait_ge(filled, 1)
                pool.wait_ge(split_done, level)
                fetch_windows(pool, far_in[k], layer, u, k, far_side(layer, u, k), far=True)

            LOAD_LAG = 5

            def divmod_unit(i, k):
                return i + k // 4, k % 4

            def reload_step(img, i, k):
                with pool.If(img < N_IMG - 1):
                    level = pool.to_reg(x_level(img, i))
                    pool.wait_ge(filled, 1)
                    pool.wait_ge(x_out[k], level)
                    following = nc.s_assert_within(img + 1, 1, N_IMG - 1, skip_runtime_bounds_check_because="only images before the last come here")
                    for b in range(BLOCKS):
                        pool.dma_start(image_block(i, k, b), dram_rows(x, following, i, k, b)).then_inc(x_in[k], DMA)

            def inverse_root(n):
                pool.wait_ge(var_eps_done, n)
                nc.gpsimd.tensor_tensor(root[:, :], var_eps[:, :], minus_half[:, :], ALU.pow).then_inc(root_done, 1)

            nc.gpsimd.memset(wrap[:, :, :], 0.0)
            nc.gpsimd.memset(windows[:, :, :, :, :], 0.0)
            for col in (0, WP - PAD):
                nc.gpsimd.memset(split[:, :, :, :, col:col + PAD], 0.0)
            nc.gpsimd.memset(ones[:, :], 1.0)
            nc.gpsimd.memset(minus_half[:, :], -0.5).then_inc(filled, 1)
            pool.wait_ge(filled, 1)

            inverse_root(1)
            with pool.Fori(0, N_IMG) as img:
                for layer in range(LAYERS):
                    if layer > 0:
                        inverse_root(img * LAYERS + layer + 1)
                    for h in range(2):
                        pad_half(img, layer, 0, 0, h)
                    if EXTRA[layer]:
                        level = pool.to_reg(edge_step(img, layer))
                        pool.wait_ge(filled, 1)
                        pool.wait_ge(low_done, level)
                        pad_columns(layer, wrap[:, :, :]).then_inc(split_done, 1)
                    far_step(img, layer, 0, 0, 0)
                    for k in range(1, 4):
                        for h in range(2):
                            if layer == 0 and k >= 2:
                                level = pool.to_reg(step(img, layer, 0, k, h))
                                pool.wait_ge(filled, 1)
                                pool.wait_ge(high_done, level)
                                for col in (0, WP - 1):
                                    nc.gpsimd.memset(split[:, k, HALF * h:HALF * h + HALF, :, col:col + 1], 0.0)
                            pad_half(img, layer, 0, k, h)
                            if layer < 3 and h == 0 and k > 1:
                                far_step(img, layer, 0, k - 1, k - 1)
                    def four_units(i, first):
                        for k in range(4):
                            for h in range(2):
                                pad_half(img, layer, i, k, h)
                                if layer < 3 and h == 0:
                                    far_step(img, layer, *((i - 1, 3, 7) if k == 0 else (i, k - 1, 4 + k - 1)))
                            if layer == 3 and not (first and k < LOAD_LAG - 4):
                                reload_step(img, *divmod_unit(i, k - LOAD_LAG))
                    four_units(1, True)
                    with pool.Fori(2, 4) as i:
                        four_units(i, False)
                    if layer < 3:
                        far_step(img, layer, 3, 3, UNITS - 1)
                    else:
                        reload_step(img, *divmod(11, 4))
                inverse_root(img * LAYERS + (LAYERS + 1))

        @block.scalar
        def _(act):
            def normalize(into, source, partitions=slice(0, P)):
                return nc.scalar.activation(into, source, ACT.Identity, bias=shift[partitions, :], scale=scale[partitions, :])

            def high_half(img, layer, i, k, h):
                source = image_half(i, k, h)
                if not (isinstance(i, int) and i == 0 and k < EARLY):
                    act.wait_ge(low_done, step(img, layer, i, k, h) - 2)
                    normalize(normed[:, step_in_layer(layer, i, k, h) % 2, :, :], source)
                normalize(split[:, k, HALF * h:HALF * h + HALF, 0, PAD:PAD + W], source).then_inc(high_done, 1)

            def high_unit(img, layer, i, k):
                act.wait_ge(conv_done, halves(img, layer, i - 1, k, 2))
                behind, k_behind = (i - 1, k + 1) if k < 3 else (i, 0)
                if far_side(layer, 4 + k_behind, k_behind) == -1:
                    act.wait_ge(far_in[k_behind], windows_level(img, layer, behind, k_behind, far_dmas))
                else:
                    act.wait_ge(windows_in[k_behind], windows_level(img, layer, behind, k_behind))
                for h in range(2):
                    high_half(img, layer, i, k, h)
                if layer == 0:
                    add_bias(img, i, k)

            def add_bias(img, i, k):
                level = act.to_reg(step(img, 0, i, k, 1))
                act.wait_ge(bands_in, DMA)
                act.wait_ge(high_done, level)
                if isinstance(i, int) and i == 0 and k < EARLY:
                    level = act.to_reg(step(img, 0, i, k, 1))
                    act.wait_ge(bands_in, DMA)
                    act.wait_ge(low_done, level)
                whole = image_half(i, k, 0, BLOCKS)
                nc.scalar.activation(whole, whole, ACT.Identity, bias=bias, scale=1.0).then_inc(bias_done, 1)

            def load_tail(img):
                following = nc.s_assert_within(img + 1, 1, N_IMG - 1, skip_runtime_bounds_check_because="only images before the last come here")
                for k in (0, 2, 3, 1):
                    if k < 2:
                        level = act.to_reg(x_level(img, 3))
                        act.wait_ge(bands_in, DMA)
                        act.wait_ge(x_out[k], level)
                    elif k == 2:
                        for side in (2, 3):
                            level = act.to_reg(windows_level(img, 3, 3, side))
                            act.wait_ge(bands_in, DMA)
                            act.wait_ge(windows_in[side], level)
                    for b in range(BLOCKS):
                        into = image_block(3, k, b) if k < 2 else waiting[k - 2][:, b * W:(b + 1) * W]
                        act.dma_start(into, dram_rows(x, following, 3, k, b)).then_inc(tail_in[k], DMA)

            act.wait_ge(bands_in, DMA)
            at = 0
            for layer in (1, 2, 3):
                nc.scalar.activation(weights[layer][:, 0, :], stage[:, at:at + W_COLS[layer]], ACT.Copy,
                                     scale=SPLIT_SCALE).then_inc(fixed_high, 1)
                at += W_COLS[layer]

            with act.Fori(0, N_IMG) as img:
                for layer in range(LAYERS):
                    act.wait_ge(dve_step, img * SMALL_STEPS + scalars_step(layer))
                    for k in range(4):
                        if layer == 0 and k >= 2:
                            with act.If(img > 0):
                                level = act.to_reg(img * DMA)
                                act.wait_ge(bands_in, DMA)
                                act.wait_ge(moved[k - 2], level)
                        high_half(img, layer, 0, k, 0)
                        if layer == 0 and k == 1:
                            act.wait_ge(top_done, img + 1)
                            nc.scalar.activation(expd[:, :], logits[:, :], ACT.Exp, bias=top[:, 1:2], scale=1.0,
                                                 accum_out=total[:, 0:1]).then_inc(exp_done, 1)
                        high_half(img, layer, 0, k, 1)
                        if layer == 0 and k >= EARLY:
                            add_bias(img, 0, k)
                        if layer == 0 and k == 1:
                            act.wait_ge(mixed_done, img + 1)
                            nc.scalar.copy(weights[0][:, 0, :], mixed_w[:, :]).then_inc(mix_high, 1)
                        if layer == 0 and k == EARLY - 1:
                            for early in range(EARLY):
                                add_bias(img, 0, early)
                        if EXTRA[layer] and k == 0:
                            edge = slice(3 * Q, 4 * Q)
                            source = image[edge, UNITS - 1, BLOCKS - 1, :]
                            normalize(wrap[edge, 0, PAD:PAD + W], source, edge).then_inc(high_done, 1)
                    with act.Fori(1, 4) as i:
                        for k in range(4):
                            high_unit(img, layer, i, k)
                with act.If(img < N_IMG - 1):
                    load_tail(img)

        @block.vector
        def _(dve):
            done = [0]

            def early_normalize(img, layer, k, h, edge=None):
                partitions = slice(0, P) if edge is None else edge
                if edge is not None:
                    dve.wait_ge(low_done, edge_step(img, layer) - 2)
                    into, source = normed[edge, 0, 0, :], image[edge, UNITS - 1, BLOCKS - 1, :]
                else:
                    if k > 0:
                        dve.wait_ge(low_done, step(img, layer, 0, k, h) - 2)
                    into, source = normed[:, step_in_layer(layer, 0, k, h) % 2, :, :], image_half(0, k, h)
                nc.vector.tensor_scalar(into, source, scale[partitions, :], shift[partitions, :],
                                        ALU.mult, ALU.add).then_inc(dve_step, 1)
                done[0] += 1
                return img * SMALL_STEPS + done[0]

            def low_half(img, layer, i, k, h):
                dve.wait_ge(high_done, step(img, layer, i, k, h))
                nc.vector.tensor_tensor(split[:, k, HALF * h:HALF * h + HALF, 1, PAD:PAD + W],
                                        normed[:, step_in_layer(layer, i, k, h) % 2, :, :],
                                        split[:, k, HALF * h:HALF * h + HALF, 0, PAD:PAD + W],
                                        ALU.subtract).then_inc(low_done, 1)

            def early_half(img, layer, k, h):
                dve.wait_ge(dve_step, early_normalize(img, layer, k, h))
                low_half(img, layer, 0, k, h)

            def first_unit(img, layer):
                normalized = [early_normalize(img, layer, 0, h) for h in range(2)]
                for h in range(2):
                    dve.wait_ge(dve_step, normalized[h])
                    low_half(img, layer, 0, 0, h)

            def statistics(i, k, h):
                v = stats[:, :, :, :].rearrange("p u b s -> p (u b) s")
                for b in range(HALF):
                    block_no = i * (4 * BLOCKS) + (k * BLOCKS + h * HALF + b)
                    last = nc.vector.bn_stats(v[:, bass.ds(block_no, 1), :].rearrange("p o s -> p (o s)"),
                                              image[:, :, :, :].rearrange("p u b w -> p (u b) w")[:, bass.ds(block_no, 1), :].rearrange("p o w -> p (o w)"))
                last.then_inc(stats_done, 1)

            def output_half(img, layer, i, k, h, ahead=None):
                dve.wait_ge(conv_done, halves(img, layer, i, k, h + 1))
                if layer == 0:
                    dve.wait_ge(bias_done, img * UNITS + i * 4 + (k + 1))
                x_half = image_half(i, k, h)
                nc.vector.scalar_tensor_tensor(x_half, psum[:, k % 2, HALF * h:HALF * h + HALF, :], 1.0 / SPLIT_SCALE ** 2,
                                               x_half, ALU.mult, ALU.add).then_inc(y_done, 1)
                if ahead is not None:
                    low_half(img, layer, *ahead, h)
                if layer < 3:
                    dve.wait_ge(y_done, halves(img, layer, i, k, h + 1))
                    statistics(i, k, h)

            def output_unit(img, layer, i, k, ahead=None):
                output_half(img, layer, i, k, 0, ahead)
                output_half(img, layer, i, k, 1, ahead)

            def last_blocks(img, layer):
                for b in (2, 3):
                    if b == 2:
                        dve.wait_ge(third_done, img * 12 + (4 * layer + 4))
                    else:
                        dve.wait_ge(conv_done, halves(img, layer, 3, 3, 2))
                    if layer == 0:
                        dve.wait_ge(bias_done, img * UNITS + UNITS)
                    x_block = image[:, UNITS - 1, b, :]
                    output = nc.vector.scalar_tensor_tensor(x_block, psum[:, 1, b, :], 1.0 / SPLIT_SCALE ** 2,
                                                            x_block, ALU.mult, ALU.add)
                    if b == 2:
                        output.then_inc(y_third_done, 1)
                        dve.wait_ge(y_third_done, img * 3 + (layer + 1))
                        nc.vector.bn_stats(stats[:, UNITS - 1, b, :], x_block)
                    else:
                        output.then_inc(y_done, 1)
                        dve.wait_ge(y_done, halves(img, layer, 3, 3, 2))
                        nc.vector.bn_stats(stats[:, UNITS - 1, b, :], x_block).then_inc(stats_done, 1)

            def next_statistics(img, *units):
                with dve.If(img < N_IMG - 1):
                    for i, k in units:
                        if isinstance(i, int) and i == 3:
                            dve.wait_ge(tail_in[k], tail_level(img))
                        else:
                            dve.wait_ge(x_in[k], x_in_level(img, i))
                        statistics(i, k, 0)
                        statistics(i, k, 1)

            def waiting_statistics(img):
                with dve.If(img < N_IMG - 1):
                    for n, k in enumerate((2, 3)):
                        dve.wait_ge(tail_in[k], tail_level(img))
                        for b in range(BLOCKS):
                            last = nc.vector.bn_stats(stats[:, UNITS - 2 + n, b, :], waiting[n][:, b * W:(b + 1) * W])
                            if b % HALF == HALF - 1:
                                last.then_inc(stats_done, 1)

            def last_statistics(img):
                with dve.If(img < N_IMG - 1):
                    dve.wait_ge(tail_in[1], tail_level(img))
                    statistics(3, 1, 0)
                    statistics(3, 1, 1)
                    level = dve.to_reg(halves(img, LAYERS, 4, 0, 0))
                    dve.wait_ge(consts_in, 3 * DMA)
                    dve.wait_ge(stats_done, level)

            def small(img, instruction):
                done[0] += 1
                instruction.then_inc(dve_step, 1)
                dve.wait_ge(dve_step, img * SMALL_STEPS + done[0])

            def partition_moments():
                nc.vector.bn_aggr(agg[:, :], stats[:, :, :, :].rearrange("p u b s -> p (u b s)")).then_inc(agg_done, 1)

            def partition_share(img, n):
                dve.wait_ge(mean_done, n)
                nc.vector.tensor_copy(mean[:, :], mean_ps)
                small(img, nc.vector.tensor_tensor(dev[:, :], agg[:, 0:1], mean_ps, ALU.subtract))
                nc.vector.scalar_tensor_tensor(var_p[:, :], dev[:, :], dev[:, :], agg[:, 1:2],
                                               ALU.mult, ALU.add).then_inc(var_p_done, 1)

            def add_eps(img, n):
                dve.wait_ge(var_done, n)
                done[0] += 1
                nc.vector.tensor_scalar(var_eps[:, :], var_ps, GROUP_EPS, 1.0 / SPLIT_SCALE ** 2, ALU.add, ALU.mult).then_inc(var_eps_done, 1)
                dve.wait_ge(var_eps_done, n)
                nc.vector.tensor_scalar(newton[:, 0:1], var_eps[:, :], -0.5, None, ALU.mult).then_inc(dve_step, 1)

            def scalars(img, n):
                dve.wait_ge(dve_step, img * SMALL_STEPS + done[0])
                dve.wait_ge(root_done, n)
                small(img, nc.vector.scalar_tensor_tensor(newton[:, 1:2], root[:, :], newton[:, 0:1], root[:, :],
                                                          ALU.mult, ALU.mult))
                small(img, nc.vector.scalar_tensor_tensor(scale[:, :], newton[:, 1:2], 1.5, root[:, :], ALU.add, ALU.mult))
                small(img, nc.vector.scalar_tensor_tensor(shift[:, :], mean[:, :], -1.0, scale[:, :],
                                                          ALU.mult, ALU.mult))

            at = 0
            for layer in (1, 2, 3):
                dve.wait_ge(fixed_high, layer)
                nc.vector.scalar_tensor_tensor(weights[layer][:, 1, :], stage[:, at:at + W_COLS[layer]], SPLIT_SCALE,
                                               weights[layer][:, 0, :], ALU.mult, ALU.subtract).then_inc(fixed_low, 1)
                at += W_COLS[layer]
            for u in range(UNITS):
                i, k = divmod(u, 4)
                dve.wait_ge(first_in[k], x_level(0, i))
                statistics(i, k, 0)
                statistics(i, k, 1)
            dve.wait_ge(consts_in, 3 * DMA)

            dve.wait_ge(stats_done, 2 * UNITS)
            partition_moments()
            partition_share(0, 1)
            add_eps(0, 1)
            scalars(0, 1)

            with dve.Fori(0, N_IMG) as img:
                for layer in range(LAYERS):
                    if layer > 0:
                        level = dve.to_reg(halves(img, layer, 4, 0, 0))
                        dve.wait_ge(consts_in, 3 * DMA)
                        dve.wait_ge(stats_done, level)
                        n = img * LAYERS + (layer + 1)
                        partition_moments()
                        partition_share(img, n)
                        add_eps(img, n)
                        scalars(img, n)
                    if layer == 0:
                        nc.vector.tensor_scalar(zed[:, :], fc_w, dev[:, :], scale[:, :], ALU.mult, ALU.mult).then_inc(zed_done, 1)
                        first_unit(img, layer)
                        dve.wait_ge(logit_done, img + 1)
                        small(img, nc.vector.scalar_tensor_tensor(logits[:, :], logit_ps, 1.0 / (SPLIT_SCALE * ROWS), fc_b,
                                                             ALU.mult, ALU.add))
                        small(img, nc.vector.reduce_max(top[:, 0:1], logits[:, :], AX.X))
                        nc.vector.tensor_scalar(top[:, 1:2], top[:, 0:1], -1.0, None, ALU.mult).then_inc(top_done, 1)
                        next_normed = early_normalize(img, layer, 1, 0)
                        dve.wait_ge(exp_done, img + 1)
                        small(img, nc.vector.reciprocal(total[:, 1:2], total[:, 0:1]))
                        small(img, nc.vector.tensor_scalar(routing[:, :], expd[:, :], total[:, 1:2], SPLIT_SCALE, ALU.mult, ALU.mult))
                        small(img, nc.vector.tensor_scalar(mixed_w[:, :], expert_w[:, 0, :], routing[:, 0:1], None, ALU.mult))
                        small(img, nc.vector.scalar_tensor_tensor(mixed_w[:, :], expert_w[:, 1, :], routing[:, 1:2], mixed_w[:, :],
                                                             ALU.mult, ALU.add))
                        nc.vector.scalar_tensor_tensor(mixed_w[:, :], expert_w[:, 2, :], routing[:, 2:3], mixed_w[:, :],
                                                       ALU.mult, ALU.add).then_inc(mixed_done, 1)
                        dve.wait_ge(dve_step, next_normed)
                        low_half(img, layer, 0, 1, 0)
                        dve.wait_ge(mix_high, img + 1)
                        nc.vector.tensor_tensor(weights[0][:, 1, :], mixed_w[:, :], weights[0][:, 0, :],
                                                ALU.subtract).then_inc(mix_low, 1)
                        early_half(img, layer, 1, 1)
                    else:
                        first_unit(img, layer)
                        if EXTRA[layer]:
                            edge = slice(3 * Q, 4 * Q)
                            dve.wait_ge(dve_step, early_normalize(img, layer, 0, 0, edge))
                            dve.wait_ge(high_done, edge_step(img, layer))
                            nc.vector.tensor_tensor(wrap[edge, 1, PAD:PAD + W], normed[edge, 0, 0, :],
                                                    wrap[edge, 0, PAD:PAD + W], ALU.subtract).then_inc(low_done, 1)
                        early_half(img, layer, 1, 0)
                        early_half(img, layer, 1, 1)
                    early_half(img, layer, 2, 0)
                    early_half(img, layer, 2, 1)

                    def four_units(i, first):
                        for k in range(4):
                            output_unit(img, layer, i, k, (i, 3) if k == 0 else (i + 1, k - 1))
                            if layer == 3 and (k >= 3 or not first):
                                next_statistics(img, (i, k - 3) if k >= 3 else (i - 1, k + 1))

                    four_units(0, True)
                    with dve.Fori(1, 3) as i:
                        four_units(i, False)
                    output_unit(img, layer, 3, 0, (3, 3))
                    if layer < 3:
                        output_unit(img, layer, 3, 1)
                        output_unit(img, layer, 3, 2)
                        output_half(img, layer, 3, 3, 0)
                        last_blocks(img, layer)
                next_statistics(img, (2, 1))
                output_unit(img, 3, 3, 1)
                next_statistics(img, (2, 2), (2, 3), (3, 0))
                output_unit(img, 3, 3, 2)
                waiting_statistics(img)
                output_unit(img, 3, 3, 3)
                last_statistics(img)
                n = img * LAYERS + (LAYERS + 1)
                partition_moments()
                partition_share(img, n)
                add_eps(img, n)
                scalars(img, n)
                assert done[0] == 5 + SMALL_STEPS

        @block.tensor
        def _(pe):
            PRODUCTS = ((0, 0), (0, 1), (1, 0))

            def inner_products(layer, k, b, q):
                w = weights[layer][:, :, :].rearrange("p s (m t n) -> p s m t n", m=3, n=Q)
                return [(w[:, w_part, q, t, :], split[:, k, b, x_part, PAD + t - 1:PAD + t - 1 + W])
                        for t in range(TAPS) for w_part, x_part in PRODUCTS]

            def outer_products(layer, k, b, q):
                w = weights[layer][:, :, :].rearrange("p s (m t n) -> p s m t n", m=3, n=Q)
                return [(w[:, w_part, 0, t, :], windows[:, k % 2, b, OUTER.index(q), PAD + t - 1:PAD + t - 1 + W])
                        for t in range(TAPS) for w_part in range(2)]

            def diagonal_products(k, b, q, whole):
                w = weights[3][:, :, 0:WINDOW_COLS].rearrange("p s (m t n) -> p s m t n", m=2, n=Q)
                own = weights[3][:, 0, WINDOW_COLS:].rearrange("p (m t n) -> p m t n", m=2, n=Q)
                first = 3 - 2 * (q % 2)
                from_block = q in INNER and not whole
                products = [(w[:, w_part, q % 2, t, :], windows[:, k % 2, b, q // 2 * 2 + x_part, first + t - 1:first + t - 1 + W])
                            for t in range(TAPS) for w_part, x_part in PRODUCTS if not (from_block and x_part)]
                if from_block:
                    products += [(own[:, INNER.index(q), t, :], split[:, k, b, 1, t:t + W]) for t in range(DIAGONAL_TAPS)]
                return products

            def multiply(k, b, products):
                last = None
                for n in range(max(len(p) for p in products.values())):
                    for q, p in products.items():
                        if n < len(p):
                            last = nc.tensor.matmul(psum[Q * q:Q * q + Q, k % 2, b, :], *p[n], start=(n == 0), stop=(n == len(p) - 1),
                                                    tile_position=(0, Q * q), skip_group_check=True)
                return last

            def inner_unit(img, layer, k):
                for h in range(2):
                    pe.wait_ge(split_done, step(img, layer, 0, k, h))
                    for b in range(HALF * h, HALF * h + HALF):
                        multiply(k, b, {q: inner_products(layer, k, b, q) for q in INNER})

            def conv_unit(img, layer, i, k, with_inner=True, whole=False):
                first = isinstance(i, int) and i == 0
                if not (first and k < 2):
                    for h in range(2):
                        pe.wait_ge(y_done, halves(img, layer, i, k - 2, h + 1))
                if with_inner and not whole:
                    pe.wait_ge(split_done, step(img, layer, i, k, 1))
                pe.wait_ge(windows_in[k], windows_level(img, layer, i, k))
                if far_side(layer, k if first else 4 + k, k) is not None:
                    pe.wait_ge(far_in[k], windows_level(img, layer, i, k, far_dmas))
                for b in range(BLOCKS):
                    if layer == 3:
                        products = {q: diagonal_products(k, b, q, whole) for q in range(4)}
                    else:
                        products = {q: outer_products(layer, k, b, q) for q in OUTER}
                        if with_inner:
                            products.update({q: inner_products(layer, k, b, q) for q in INNER})
                    last = multiply(k, b, products)
                    if b % HALF == HALF - 1:
                        last.then_inc(conv_done, 1)
                    elif layer < 3 and k == 3 and b == 2:
                        last.then_inc(third_done, 1)

            def group_averages(n):
                pe.wait_ge(agg_done, n)
                nc.tensor.matmul(mean_ps, group_avg[:, :], agg[:, 0:1], start=True, stop=True).then_inc(mean_done, 1)
                pe.wait_ge(var_p_done, n)
                nc.tensor.matmul(var_ps, group_avg[:, :], var_p[:, :], start=True, stop=True).then_inc(var_done, 1)

            group_averages(1)
            with pe.Fori(0, N_IMG) as img:
                for layer in range(LAYERS):
                    if layer == 0:
                        pe.wait_ge(zed_done, img + 1)
                        nc.tensor.matmul(logit_ps, ones[:, :], zed[:, :], start=True, stop=True).then_inc(logit_done, 1)
                        pe.wait_ge(mix_low, img + 1)
                    else:
                        group_averages(img * LAYERS + (layer + 1))
                    pe.wait_ge(dve_step, img * SMALL_STEPS + scalars_step(layer))
                    if layer < 3:
                        inner_unit(img, layer, 0)
                        inner_unit(img, layer, 1)
                    for k in range(4):
                        conv_unit(img, layer, 0, k, with_inner=layer == 3 or k >= 2)
                    with pe.Fori(1, 4 if layer < 3 else 3) as i:
                        for k in range(4):
                            conv_unit(img, layer, i, k)
                    if layer == 3:
                        for k in range(4):
                            conv_unit(img, layer, 3, k, whole=12 + k >= WHOLE_FROM)
                pe.wait_ge(y_done, halves(img, 3, 3, 3, 0))
                group_averages(img * LAYERS + (LAYERS + 1))
                pe.wait_ge(y_done, halves(img, 3, 3, 3, 2))


def lay_out(L0_conv_w_experts, L0_conv_bias, L0_conv_fc_w, L0_conv_fc_b, L1_conv_weight, L2_conv_weight, L3_conv_filter_w):
    import numpy as np

    def window(w):
        m = np.zeros((2, 4, C, TAPS, 2, C), np.float32)
        for out_row in range(2):
            for kh in range(3):
                m[:, out_row + kh, :, :, out_row, :] = w[:, :, kh, :].transpose(1, 2, 0)
        return m.reshape(P, TAPS * Q)

    def inner(w, q):
        m = np.zeros((ROWS, C, TAPS, 2, C), np.float32)
        for out_row in range(2):
            for kh in range(3):
                m[2 * q + out_row + kh - 1, :, :, out_row, :] = w[:, :, kh, :].transpose(1, 2, 0)
        return m.reshape(P, TAPS * Q)

    def square(w):
        return np.concatenate([window(w)] + [inner(w, q) for q in INNER], axis=1)

    def diagonal(f):
        m = np.zeros((4, 2, C, 2, TAPS, 2, C), np.float32)
        for g in range(4):
            for row in range(2):
                for place in range(2):
                    for out_row in range(2):
                        tap = 2 * (g - 1 - place) + row - out_row
                        if -2 <= tap <= 2:
                            m[g, row, :, place, row - out_row + 1, out_row, :] = f[:, :, tap + 2].T
        own = np.zeros((ROWS, C, 2, DIAGONAL_TAPS, 2, C), np.float32)
        for n, q in enumerate(INNER):
            for tap in range(DIAGONAL_TAPS):
                for out_row in range(2):
                    own[2 * q + out_row + tap - 2, :, n, tap, out_row, :] = f[:, :, tap].T
        return np.concatenate([m.reshape(P, WINDOW_COLS), own.reshape(P, DIAGONAL_COLS - WINDOW_COLS)], axis=1)

    experts = np.stack([square(w) for w in L0_conv_w_experts], axis=1)
    bands = np.concatenate([square(L1_conv_weight[:, :, ::-1, ::-1]), square(L2_conv_weight[:, :, ::-1, ::-1]),
                            diagonal(L3_conv_filter_w)], axis=1)
    partition = np.arange(P)
    group = (partition % C) // 2
    group_avg = np.where(group[:, None] == group[None, :], np.float32(1.0 / (P // (C // 2))), np.float32(0.0))
    small = np.zeros((P, 2 * EXPERTS + 1), np.float32)
    for r in range(ROWS):
        small[C * r:C * r + C, 0:EXPERTS] = L0_conv_fc_w.T
        small[C * r:C * r + C, EXPERTS:2 * EXPERTS] = L0_conv_fc_b
        small[C * r:C * r + C, 2 * EXPERTS] = L0_conv_bias
    return np.ascontiguousarray(experts), np.ascontiguousarray(bands), group_avg, small


def kernel(x, L0_conv_w_experts, L0_conv_bias, L0_conv_fc_w, L0_conv_fc_b, L1_conv_weight, L2_conv_weight, L3_conv_filter_w):
    import numpy as np
    import concourse.bacc as bacc
    from concourse.bass_utils import run_bass_kernel_spmd

    weights = [np.asarray(a) for a in (L0_conv_w_experts, L0_conv_bias, L0_conv_fc_w, L0_conv_fc_b,
                                       L1_conv_weight, L2_conv_weight, L3_conv_filter_w)]
    experts, bands, group_avg, small = lay_out(*weights)
    arrays = {"x": np.ascontiguousarray(x), "experts": experts, "bands": bands, "group_avg": group_avg, "small": small}
    nc = bacc.Bacc("TRN2", target_bir_lowering=False, num_devices=1, dynamic_dma_scratch_size=SCRATCH)
    aps = [nc.dram_tensor(n, a.shape, mybir.dt.from_np(a.dtype), kind="ExternalInput").ap() for n, a in arrays.items()]
    out = nc.dram_tensor("out", (N_IMG, C, H, W), mybir.dt.float32, kind="ExternalOutput").ap()
    build(nc, *aps, out)
    result = run_bass_kernel_spmd(nc, [arrays], core_ids=[0])
    return result.results[0]["out"]
```
